# Optimizing a Trainium2 kernel written in Bass

```python
import numpy as np
import jax
import jax.numpy as jnp

def _softmax(x, axis=-1):
    return jax.nn.softmax(x, axis=axis)

def _gelu(x):
    return jax.nn.gelu(x, approximate=True)

def _silu(x):
    return jax.nn.silu(x)

def _sigmoid(x):
    return jax.nn.sigmoid(x)

def _layernorm(x, axis=-1, eps=1e-05):
    m = jnp.mean(x, axis=axis, keepdims=True)
    v = jnp.var(x, axis=axis, keepdims=True)
    return (x - m) / jnp.sqrt(v + eps)

def _scatter_add(tgt, idx, src, axis=0):
    return tgt.at[idx].add(src)

def _segment_sum(src, seg, n):
    return jax.ops.segment_sum(src, seg, n)
kernel_name = 'mk_flamingo_gated_d2_seqx_r4_0b75fa'

def setup_inputs(seed: int=0):
    np.random.seed(seed)
    _w = jnp.asarray

    def _rec_inputs():
        import jax
        import jax.numpy as jnp
        _rk = jax.random.key(seed)
        x = 7.22e-05 + 1 * jax.random.normal(jax.random.fold_in(_rk, 1), (2, 1024, 256), jnp.float32)
        _lenS = 1024 - jax.random.randint(jax.random.fold_in(_rk, 7), (2,), 0, max(1, 1024 // 4) + 1, jnp.int32)
        _lenS2 = 77 - jax.random.randint(jax.random.fold_in(_rk, 8), (2,), 0, max(1, 77 // 4) + 1, jnp.int32)
        _ctx_1024P = jax.random.normal(jax.random.fold_in(_rk, 11), (2, 16, 256), jnp.float32)
        _ctx_1024c = jax.random.dirichlet(jax.random.fold_in(_rk, 511), 0.3 * jnp.ones((16,), jnp.float32), (2, 77))
        _ctx_1024t = jnp.einsum('bsk,bkd->bsd', _ctx_1024c, _ctx_1024P)
        _ctx_1024t = _ctx_1024t * jax.lax.rsqrt(jnp.mean(jnp.square(_ctx_1024t)) + 1e-12) * 0.953939
        ctx_1024 = 4.13588e-05 + 0.999923 * (_ctx_1024t + 0.3 * jax.random.normal(jax.random.fold_in(_rk, 611), (2, 77, 256), jnp.float32))
        _validS = jnp.arange(1024)[None, :] < _lenS[:, None]
        _validS2 = jnp.arange(77)[None, :] < _lenS2[:, None]
        _causal = jnp.tril(jnp.ones((1024, 1024), dtype=bool))
        mask_BxSxS2_bk1 = jnp.broadcast_to(_validS2[:, None, :], (2, 1024, 77))
        mask_BxS2_bk1 = jnp.broadcast_to(_validS2[:, :], (2, 77))
        _g = jax.random.normal(jax.random.fold_in(_rk, 9001), (2, 2), jnp.float32)
        _g = jnp.sign(_g) * jnp.maximum(jnp.abs(_g), 1.0) + (_g == 0) * 1.0
        g_xattn = _g[0]
        g_ffn = _g[1]
        return (x, ctx_1024, mask_BxSxS2_bk1, mask_BxS2_bk1, g_xattn, g_ffn)
    x, ctx_1024, mask_BxSxS2_bk1, mask_BxS2_bk1, g_xattn, g_ffn = _rec_inputs()

    def _L0_xattn_setup():
        import jax, jax.numpy as jnp
        import numpy as np
        HIDDEN = 256
        NUM_HEADS = 16
        DK = 64
        DV = 64
        NEG_INF = -1000000000.0
        key = jax.random.key(seed)
        ks = jax.random.split(key, 12)
        B, S = (4, 512)
        scale = 0.02
        return {'q_hidden_inputs': jax.random.normal(ks[0], (B, S, HIDDEN), dtype=jnp.float32), 'k_hidden_inputs': jax.random.normal(ks[1], (B, S, HIDDEN), dtype=jnp.float32), 'v_hidden_inputs': jax.random.normal(ks[2], (B, S, HIDDEN), dtype=jnp.float32), 'mask': jax.random.randint(ks[3], (B, S, S), 0, 2) > 0, 'wq': jax.random.normal(ks[4], (NUM_HEADS, HIDDEN, DK), dtype=jnp.float32) * scale, 'bq': jax.random.normal(ks[5], (NUM_HEADS, DK), dtype=jnp.float32) * scale, 'wk': jax.random.normal(ks[6], (NUM_HEADS, HIDDEN, DK), dtype=jnp.float32) * scale, 'bk': jax.random.normal(ks[7], (NUM_HEADS, DK), dtype=jnp.float32) * scale, 'wv': jax.random.normal(ks[8], (NUM_HEADS, HIDDEN, DV), dtype=jnp.float32) * scale, 'bv': jax.random.normal(ks[9], (NUM_HEADS, DV), dtype=jnp.float32) * scale, 'wo': jax.random.normal(ks[10], (NUM_HEADS * DV, HIDDEN), dtype=jnp.float32) * scale, 'bo': jax.random.normal(ks[11], (HIDDEN,), dtype=jnp.float32) * scale}
    _L0_xattn_all = _L0_xattn_setup()
    _L0_xattn_in = {k: v for k, v in _L0_xattn_all.items() if k in ('wq', 'bq', 'wk', 'bk', 'wv', 'bv', 'wo', 'bo')}
    del _L0_xattn_all

    def _L0_ffn_setup():
        import jax, jax.numpy as jnp
        import numpy as np
        B, S, DIM = (4, 1024, 256)
        BASE_COUPLING = 0.1
        NUM_CYCLES = 3

        def _gelu(x):
            return jax.nn.gelu(x, approximate=False)

        def _coupling_net(h, w1, b1, w2, b2, w3, b3, w4, b4):
            h = _gelu(h @ w1 + b1)
            h = _gelu(h @ w2 + b2)
            h = _gelu(h @ w3 + b3)
            return jax.nn.sigmoid(h @ w4 + b4)

        def _global_net(h, w1, b1, w2, b2, w3, b3):
            h = _gelu(h @ w1 + b1)
            h = _gelu(h @ w2 + b2)
            return jax.nn.sigmoid(h @ w3 + b3)

        def _twist(x):
            o_r, o_i, p_r, p_i = jnp.split(x, 4, axis=-1)
            return jnp.concatenate([p_r, -p_i, -o_r, o_i], axis=-1)
        key = jax.random.key(seed)
        ks = jax.random.split(key, 9)
        d = DIM

        def w(k, fan_in, fan_out):
            return jax.random.normal(k, (fan_in, fan_out), dtype=jnp.float32) / np.sqrt(fan_in).astype(np.float32)
        inp = {'x': jax.random.normal(ks[0], (B, S, d), dtype=jnp.float32)}
        cn_dims = [(d, d), (d, d // 2), (d // 2, d // 4), (d // 4, 1)]
        for i, (a, b) in enumerate(cn_dims):
            inp[f'cn_w{i + 1}'] = w(ks[1 + i], a, b)
            inp[f'cn_b{i + 1}'] = jnp.zeros((b,), dtype=jnp.float32)
        gc_dims = [(d, d // 2), (d // 2, d // 4), (d // 4, 1)]
        for i, (a, b) in enumerate(gc_dims):
            inp[f'gc_w{i + 1}'] = w(ks[5 + i], a, b)
            inp[f'gc_b{i + 1}'] = jnp.zeros((b,), dtype=jnp.float32)
        inp['adaptive_range'] = jnp.full((1,), 0.2, dtype=jnp.float32)
        return inp
    _L0_ffn_all = _L0_ffn_setup()
    _L0_ffn_in = {k: v for k, v in _L0_ffn_all.items() if k in ('cn_w1', 'cn_b1', 'cn_w2', 'cn_b2', 'cn_w3', 'cn_b3', 'cn_w4', 'cn_b4', 'gc_w1', 'gc_b1', 'gc_w2', 'gc_b2', 'gc_w3', 'gc_b3', 'adaptive_range')}
    del _L0_ffn_all

    def _L1_xattn_setup():
        import jax, jax.numpy as jnp
        import numpy as np
        B, S, T, D, H = (4, 512, 512, 256, 16)
        HD = D // H
        key = jax.random.key(seed)
        ks = jax.random.split(key, 7)
        src = jax.random.normal(ks[0], (B, S, D), dtype=jnp.float32)
        tgt = jax.random.normal(ks[1], (B, T, D), dtype=jnp.float32)
        attention_mask = jax.random.bernoulli(ks[2], 0.9, (B, S))
        scale = 1.0 / np.sqrt(D)
        Wq = jax.random.normal(ks[3], (D, D), dtype=jnp.float32) * scale
        Wk = jax.random.normal(ks[4], (D, D), dtype=jnp.float32) * scale
        Wv = jax.random.normal(ks[5], (D, D), dtype=jnp.float32) * scale
        Wo = jax.random.normal(ks[6], (D, D), dtype=jnp.float32) * scale
        return {'src': src, 'tgt': tgt, 'attention_mask': attention_mask, 'Wq': Wq, 'Wk': Wk, 'Wv': Wv, 'Wo': Wo}
    _L1_xattn_all = _L1_xattn_setup()
    _L1_xattn_in = {k: v for k, v in _L1_xattn_all.items() if k in ('Wq', 'Wk', 'Wv', 'Wo')}
    del _L1_xattn_all

    def _L1_ffn_setup():
        import jax, jax.numpy as jnp
        import numpy as np
        D_MODEL = 256
        NUM_EXPERTS = 8
        HIDDEN = 512
        TOP_K = 2
        SHARED_HIDDEN = 512
        BATCH, SEQ = (4, 512)
        key = jax.random.key(seed)
        ks = jax.random.split(key, 8)
        s = 1.0 / np.sqrt(D_MODEL)
        sh = 1.0 / np.sqrt(HIDDEN)
        return {'x': jax.random.normal(ks[0], (BATCH, SEQ, D_MODEL), dtype=jnp.float32), 'w_router': jax.random.normal(ks[1], (D_MODEL, NUM_EXPERTS), dtype=jnp.float32) * s, 'w1': jax.random.normal(ks[2], (NUM_EXPERTS, D_MODEL, HIDDEN), dtype=jnp.float32) * s, 'w3': jax.random.normal(ks[3], (NUM_EXPERTS, D_MODEL, HIDDEN), dtype=jnp.float32) * s, 'w2': jax.random.normal(ks[4], (NUM_EXPERTS, HIDDEN, D_MODEL), dtype=jnp.float32) * sh, 'ws1': jax.random.normal(ks[5], (D_MODEL, SHARED_HIDDEN), dtype=jnp.float32) * s, 'ws3': jax.random.normal(ks[6], (D_MODEL, SHARED_HIDDEN), dtype=jnp.float32) * s, 'ws2': jax.random.normal(ks[7], (SHARED_HIDDEN, D_MODEL), dtype=jnp.float32) * sh}
    _L1_ffn_all = _L1_ffn_setup()
    _L1_ffn_in = {k: v for k, v in _L1_ffn_all.items() if k in ('w_router', 'w1', 'w3', 'w2', 'ws1', 'ws3', 'ws2')}
    del _L1_ffn_all
    return {'x': x, 'ctx_1024': ctx_1024, 'mask_BxSxS2_bk1': mask_BxSxS2_bk1, 'mask_BxS2_bk1': mask_BxS2_bk1, 'g_xattn': g_xattn, 'g_ffn': g_ffn, 'L0_xattn_wq': _L0_xattn_in['wq'], 'L0_xattn_bq': _L0_xattn_in['bq'], 'L0_xattn_wk': _L0_xattn_in['wk'], 'L0_xattn_bk': _L0_xattn_in['bk'], 'L0_xattn_wv': _L0_xattn_in['wv'], 'L0_xattn_bv': _L0_xattn_in['bv'], 'L0_xattn_wo': _L0_xattn_in['wo'], 'L0_xattn_bo': _L0_xattn_in['bo'], 'L0_ffn_cn_w1': _L0_ffn_in['cn_w1'], 'L0_ffn_cn_b1': _L0_ffn_in['cn_b1'], 'L0_ffn_cn_w2': _L0_ffn_in['cn_w2'], 'L0_ffn_cn_b2': _L0_ffn_in['cn_b2'], 'L0_ffn_cn_w3': _L0_ffn_in['cn_w3'], 'L0_ffn_cn_b3': _L0_ffn_in['cn_b3'], 'L0_ffn_cn_w4': _L0_ffn_in['cn_w4'], 'L0_ffn_cn_b4': _L0_ffn_in['cn_b4'], 'L0_ffn_gc_w1': _L0_ffn_in['gc_w1'], 'L0_ffn_gc_b1': _L0_ffn_in['gc_b1'], 'L0_ffn_gc_w2': _L0_ffn_in['gc_w2'], 'L0_ffn_gc_b2': _L0_ffn_in['gc_b2'], 'L0_ffn_gc_w3': _L0_ffn_in['gc_w3'], 'L0_ffn_gc_b3': _L0_ffn_in['gc_b3'], 'L0_ffn_adaptive_range': _L0_ffn_in['adaptive_range'], 'L1_xattn_Wq': _L1_xattn_in['Wq'], 'L1_xattn_Wk': _L1_xattn_in['Wk'], 'L1_xattn_Wv': _L1_xattn_in['Wv'], 'L1_xattn_Wo': _L1_xattn_in['Wo'], 'L1_ffn_w_router': _L1_ffn_in['w_router'], 'L1_ffn_w1': _L1_ffn_in['w1'], 'L1_ffn_w3': _L1_ffn_in['w3'], 'L1_ffn_w2': _L1_ffn_in['w2'], 'L1_ffn_ws1': _L1_ffn_in['ws1'], 'L1_ffn_ws3': _L1_ffn_in['ws3'], 'L1_ffn_ws2': _L1_ffn_in['ws2']}

def reference(x, ctx_1024, mask_BxSxS2_bk1, mask_BxS2_bk1, g_xattn, g_ffn, L0_xattn_wq, L0_xattn_bq, L0_xattn_wk, L0_xattn_bk, L0_xattn_wv, L0_xattn_bv, L0_xattn_wo, L0_xattn_bo, L0_ffn_cn_w1, L0_ffn_cn_b1, L0_ffn_cn_w2, L0_ffn_cn_b2, L0_ffn_cn_w3, L0_ffn_cn_b3, L0_ffn_cn_w4, L0_ffn_cn_b4, L0_ffn_gc_w1, L0_ffn_gc_b1, L0_ffn_gc_w2, L0_ffn_gc_b2, L0_ffn_gc_w3, L0_ffn_gc_b3, L0_ffn_adaptive_range, L1_xattn_Wq, L1_xattn_Wk, L1_xattn_Wv, L1_xattn_Wo, L1_ffn_w_router, L1_ffn_w1, L1_ffn_w3, L1_ffn_w2, L1_ffn_ws1, L1_ffn_ws3, L1_ffn_ws2):
    import jax
    import jax.numpy as jnp

    def _L0_xattn_ref(q_hidden_inputs, k_hidden_inputs, v_hidden_inputs, mask, wq, bq, wk, bk, wv, bv, wo, bo):
        import jax, jax.numpy as jnp
        import numpy as np
        HIDDEN = 256
        NUM_HEADS = 16
        DK = 64
        DV = 64
        NEG_INF = -1000000000.0
        q = jnp.einsum('bsd,hdk->bhsk', q_hidden_inputs, wq) + bq[None, :, None, :]
        k = jnp.einsum('bsd,hdk->bhsk', k_hidden_inputs, wk) + bk[None, :, None, :]
        v = jnp.einsum('bsd,hdv->bhsv', v_hidden_inputs, wv) + bv[None, :, None, :]
        scores = jnp.einsum('bhsk,bhtk->bhst', q, k) / jnp.sqrt(jnp.float32(DK))
        scores = jnp.where(mask[:, None, :, :], scores, NEG_INF)
        attn = jax.nn.softmax(scores, axis=-1)
        out = jnp.einsum('bhst,bhtv->bhsv', attn, v)
        B, H, Sq, Dv = out.shape
        out = jnp.transpose(out, (0, 2, 1, 3)).reshape(B, Sq, H * Dv)
        return out @ wo + bo

    def _L0_ffn_ref(x, cn_w1, cn_b1, cn_w2, cn_b2, cn_w3, cn_b3, cn_w4, cn_b4, gc_w1, gc_b1, gc_w2, gc_b2, gc_w3, gc_b3, adaptive_range):
        import jax, jax.numpy as jnp
        import numpy as np
        B, S, DIM = (4, 1024, 256)
        BASE_COUPLING = 0.1
        NUM_CYCLES = 3

        def _gelu(x):
            return jax.nn.gelu(x, approximate=False)

        def _coupling_net(h, w1, b1, w2, b2, w3, b3, w4, b4):
            h = _gelu(h @ w1 + b1)
            h = _gelu(h @ w2 + b2)
            h = _gelu(h @ w3 + b3)
            return jax.nn.sigmoid(h @ w4 + b4)

        def _global_net(h, w1, b1, w2, b2, w3, b3):
            h = _gelu(h @ w1 + b1)
            h = _gelu(h @ w2 + b2)
            return jax.nn.sigmoid(h @ w3 + b3)

        def _twist(x):
            o_r, o_i, p_r, p_i = jnp.split(x, 4, axis=-1)
            return jnp.concatenate([p_r, -p_i, -o_r, o_i], axis=-1)
        global_context = x.mean(axis=1, keepdims=True)
        gf = _global_net(global_context, gc_w1, gc_b1, gc_w2, gc_b2, gc_w3, gc_b3)
        out = x
        for _ in range(NUM_CYCLES):
            tf = _coupling_net(out, cn_w1, cn_b1, cn_w2, cn_b2, cn_w3, cn_b3, cn_w4, cn_b4)
            combined = 0.7 * gf + 0.3 * tf
            coupling = BASE_COUPLING + adaptive_range * (combined - 0.5) * 2.0
            out = out + coupling * _twist(out)
        return out

    def _L1_xattn_ref(src, tgt, attention_mask, Wq, Wk, Wv, Wo):
        import jax, jax.numpy as jnp
        import numpy as np
        B, S, T, D, H = (4, 512, 512, 256, 16)
        HD = D // H
        b, s, d = src.shape
        t = tgt.shape[1]
        q = (tgt @ Wq.T).reshape(b, t, H, HD).transpose(0, 2, 1, 3)
        k = (src @ Wk.T).reshape(b, s, H, HD).transpose(0, 2, 1, 3)
        v = (src @ Wv.T).reshape(b, s, H, HD).transpose(0, 2, 1, 3)
        scores = jnp.einsum('bhtd,bhsd->bhts', q, k) / np.sqrt(HD)
        mask = attention_mask[:, None, None, :]
        scores = jnp.where(mask, scores, -jnp.inf)
        attn = jax.nn.softmax(scores, axis=-1)
        out = jnp.einsum('bhts,bhsd->bhtd', attn, v)
        out = out.transpose(0, 2, 1, 3).reshape(b, t, d)
        return out @ Wo.T

    def _L1_ffn_ref(x, w_router, w1, w3, w2, ws1, ws3, ws2):
        import jax, jax.numpy as jnp
        import numpy as np
        D_MODEL = 256
        NUM_EXPERTS = 8
        HIDDEN = 512
        TOP_K = 2
        SHARED_HIDDEN = 512
        BATCH, SEQ = (4, 512)
        orig_shape = x.shape
        xf = x.reshape(-1, D_MODEL)
        T = xf.shape[0]
        logits = xf @ w_router
        scores = jax.nn.softmax(logits, axis=-1)
        expert_weights, expert_indices = jax.lax.top_k(scores, TOP_K)
        cw = jnp.zeros((T, NUM_EXPERTS), dtype=xf.dtype)
        cw = cw.at[jnp.arange(T)[:, None], expert_indices].add(expert_weights)
        h = jax.nn.silu(jnp.einsum('td,edh->teh', xf, w1)) * jnp.einsum('td,edh->teh', xf, w3)
        y = jnp.einsum('teh,ehd->ted', h, w2)
        moe_out = jnp.einsum('te,ted->td', cw, y)
        shared = jax.nn.silu(xf @ ws1) * (xf @ ws3) @ ws2
        out = shared / (TOP_K + 1) + moe_out * (TOP_K / (TOP_K + 1))
        return out.reshape(orig_shape)
    x = x + jnp.tanh(g_xattn[0]) * _L0_xattn_ref(_layernorm(x, axis=-1), ctx_1024, ctx_1024, mask_BxSxS2_bk1, L0_xattn_wq, L0_xattn_bq, L0_xattn_wk, L0_xattn_bk, L0_xattn_wv, L0_xattn_bv, L0_xattn_wo, L0_xattn_bo)
    x = x + jnp.tanh(g_ffn[0]) * _L0_ffn_ref(_layernorm(x, axis=-1), L0_ffn_cn_w1, L0_ffn_cn_b1, L0_ffn_cn_w2, L0_ffn_cn_b2, L0_ffn_cn_w3, L0_ffn_cn_b3, L0_ffn_cn_w4, L0_ffn_cn_b4, L0_ffn_gc_w1, L0_ffn_gc_b1, L0_ffn_gc_w2, L0_ffn_gc_b2, L0_ffn_gc_w3, L0_ffn_gc_b3, L0_ffn_adaptive_range)
    x = x + jnp.tanh(g_xattn[1]) * _L1_xattn_ref(ctx_1024, _layernorm(x, axis=-1), mask_BxS2_bk1, L1_xattn_Wq, L1_xattn_Wk, L1_xattn_Wv, L1_xattn_Wo)
    x = x + jnp.tanh(g_ffn[1]) * _L1_ffn_ref(_layernorm(x, axis=-1), L1_ffn_w_router, L1_ffn_w1, L1_ffn_w3, L1_ffn_w2, L1_ffn_ws1, L1_ffn_ws3, L1_ffn_ws2)
    return x

_drawn_inputs = setup_inputs


def setup_inputs(seed=0):
    import zlib

    import numpy as np

    out = dict(_drawn_inputs(seed))
    spreads = {'g_ffn': (-1.0, 0.554),
     'L0_ffn_cn_b1': (0.0, 0.8),
     'L0_ffn_cn_b2': (0.0, 2.0),
     'L0_ffn_cn_b3': (0.0, 0.713),
     'L0_ffn_gc_b1': (0.0, 0.785),
     'L0_ffn_gc_b2': (0.0, 0.47)}
    factors = {'L0_xattn_wq': 8.0,
     'L0_xattn_bq': 23.801,
     'L0_xattn_wk': 8.0,
     'L0_xattn_bk': 64.0,
     'L0_xattn_bv': 4.321,
     'L0_xattn_bo': 3.376,
     'L0_ffn_gc_w1': 5.345,
     'L0_ffn_gc_w2': 4.46}
    for name, (base, spread) in spreads.items():
        noise = np.random.default_rng([zlib.crc32(name.encode()), seed]).standard_normal(out[name].shape)
        drawn = base * np.exp(spread * noise) if base else spread * noise
        out[name] = jnp.asarray(drawn.astype(out[name].dtype))
    for name, factor in factors.items():
        out[name] = (out[name] * factor).astype(out[name].dtype)
    return out
```

```python
from contextlib import ExitStack

import concourse.bass as bass
from concourse import mybir

P = 128
B, S, D = 2, 1024, 256
T = B * S // P
TB = T // B
KD = D // P
NK = 77
H = 16
DK = 64
HD = D // H
PAIRS = H // 2
PW = 2 * NK
HK = H * NK
HALF = HK // 2
KC = (HK + P - 1) // P
LASTK = HK - (KC - 1) * P
BO_ROW = 96
UNITS = [(0, 6), (6, 12), (12, 16)]
PTG = [(0, 4), (4, 8), (8, KC)]
ZS = PW + P
ZN = PAIRS * ZS + P
ZL = 104
Z1 = ZL + HALF + 48
G4 = 512
NG = B * S // G4
NE = 8
F = 512
FC = F // P
SLOTS = 2 * B * S // P + NE - 1
EPS = 1e-5
BIG = 1e30

F32 = mybir.dt.float32
BF16 = mybir.dt.bfloat16
I32 = mybir.dt.int32
U32 = mybir.dt.uint32
ALU = mybir.AluOpType
ACT = mybir.ActivationFunctionType
AX = mybir.AxisListType

C_ID = 0
C_UP = C_ID + P
C_BD = C_UP + P
C_IN = C_BD + 8
C_RE = C_IN + KC * 3
C_TH = C_RE + NE
C_SL = C_TH + T
C_SG = C_SL + SLOTS
C_N = C_SG + 1

V_GX, V_GF, V_AR, V_GB3, V_CB4 = 0, 2, 4, 5, 6
V_CB1, V_CB2, V_CB3, V_GB1, V_GB2 = 7, 9, 10, 11, 12
V_BK, V_BV, V_BQ = 13, 21, 29
V_N = 37


def heads_of(c):
    last = min(c * P + P, HK) - 1
    return c * P // NK, last // NK - c * P // NK + 1


class Chain:

    def __init__(self, eng, sem):
        self.eng, self.sem, self.base, self.n = eng, sem, 0, 0

    def __call__(self, ins):
        ins.then_inc(self.sem, 1)
        self.n += 1
        self.eng.wait_ge(self.sem, self.base + self.n)

    def mark(self, ins):
        ins.then_inc(self.sem, 1)
        self.n += 1

    def sync(self):
        self.eng.wait_ge(self.sem, self.base + self.n)

    def enter(self, turn, each):
        self.at = self.n + (self.base if isinstance(self.base, int) else 0)
        self.base, self.n, self.each = self.at + turn * each, 0, each

    def leave(self, turns):
        assert self.n == self.each, (self.n, self.each)
        self.base, self.n = self.at + turns * self.each, 0


def after(eng, sem, value):
    if not isinstance(value, int) or value > 0:
        eng.wait_ge(sem, value)


def halves_of(c):
    h0, n = heads_of(c)
    return sorted({h0 // 8, (h0 + n - 1) // 8})


def spread(ap, axis, shape):
    return ap.unsqueeze(axis).to_broadcast(shape)


def build(nc, x, ctxT, maskT, mask1, consts, small, wk0, wv0, wq0T, wo0, bo0, cw1, cw2, cw3, cw4,
          gw1, gw2, gw3, wq1, wk1, wv1, wo1, wr, w1, w3, w2, ws1, ws3, ws2, out, dbg=None):
    st = ExitStack()
    with st:
        def sb(name, cols, dt=F32, rows=P):
            return st.enter_context(nc.sbuf_tensor(name, [rows] + (cols if isinstance(cols, list) else [cols]), dt))

        def sem(name):
            return st.enter_context(nc.semaphore(name))

        ps = st.enter_context(nc.psum_tensor("ps", [P, 8, 512], F32))

        xs = sb("x_rows", [T, D])
        con = sb("consts_sb", C_N)
        par = sb("params_sb", V_N)
        ctx = sb("ctx_sb", [KD, B * NK])
        early = sb("early", 2 * NE * KD * F)
        middle = sb("middle", NE * FC * D + T * D)
        work = sb("work", 7424)
        late = sb("late", 7168)
        mrow_u8 = sb("mask_row_u8", [B, NK], mybir.dt.uint8, 1)
        mrf = sb("mask_row_f", [B, NK], rows=1); mval = sb("mask_valid", [4], rows=1)
        masks = sb("masks", 4 * HK // 2 + B * S // 2 + B * S // 4)
        stats = sb("stats", [T, 6]); mv = sb("mean_var", [T, 2])
        vare = sb("var_eps", T); rstd = sb("rstd", T); mhalf = sb("minus_half", T)
        mx = sb("maxes", H); den = sb("den", H); rden = sb("rden", H)
        gate = sb("gates", 4); gw = sb("gate_work", 8)
        ones_bf = sb("ones_bf", P, BF16)
        up_bf = sb("upper_bf", P, BF16)
        csum = sb("feature_sums", [KD, NG])
        gcx = sb("gc_x", [KD, B]); gh1 = sb("gc_h1", B); gh2 = sb("gc_h2", B, rows=64); gtan = sb("gc_tanh", B)
        cpl = sb("coupling", 4); hb = sb("half_biases", 2)

        def cut(region, at, shape):
            n = 1
            for s in shape:
                n *= s
            v = region[:, at:at + n]
            if len(shape) == 1:
                return v
            names = "abcd"[:len(shape)]
            return v.rearrange(f"p ({' '.join(names)}) -> p {' '.join(names)}", **dict(zip(names[1:], shape[1:])))

        ident = con[:, C_ID:C_ID + P]
        wk_s = cut(early, 0, [KD, H * DK]); wv_s = cut(early, 2048, [KD, H * DK])
        wq_s = cut(early, 4096, [PAIRS, D]); wo_s = cut(early, 6144, [PAIRS, D])
        kbd = cut(early, 8192, [B, PAIRS, PW])
        zv = cut(early, 8192 + B * PAIRS * PW, [B, ZN])
        z1 = cut(early, 0, [B, 2, Z1])
        w13 = cut(early, 0, [NE, 2, KD, F])
        gk = cut(middle, 0, [B, KD, HK])
        vo = cut(middle, B * KD * HK, [B, KC, D])
        st_x = cut(middle, 0, [KD, NG, G4])
        h1 = [cut(middle, 4096 + 1024 * p, [2, G4]) for p in range(2)]
        h2 = [cut(middle, 6144 + 512 * p, [G4]) for p in range(2)]
        h3 = [cut(middle, 7168 + 512 * p, [G4]) for p in range(2)]
        tt = [cut(middle, 8192 + 512 * p, [G4]) for p in range(2)]
        cs = cut(middle, 9216, [G4]); u0 = cut(middle, 9728, [G4]); u1 = cut(middle, 10240, [G4])
        w2s = cut(middle, 0, [NE, FC, D])
        xn4 = cut(middle, NE * FC * D, [T, D])
        xn = [cut(work, 256 * p, [D]) for p in range(2)]
        xnT = [cut(work, 512 + 256 * p, [KD, P]) for p in range(2)]
        qT = [cut(work, 1024 + 256 * p, [KD, P]) for p in range(2)]
        sc = [cut(work, 1536 + HK * p, [HK]) for p in range(2)]
        pt = [cut(work, 4000 + KC * P * p, [KC, P]) for p in range(2)]
        att = cut(work, 6560, [D]); attT = cut(work, 6816, [KD, P])
        h = HK // 2
        mrhs = [masks[0:80, h * b:h * b + h].bitcast(BF16) for b in range(B)]
        mrow = [masks[0:1, h * (2 + b):h * (3 + b)].bitcast(BF16) for b in range(B)]
        mlhs = masks[0:80, 4 * h:4 * h + B * S // 2].bitcast(BF16).rearrange("p (b s) -> p b s", b=B)
        mask_u8 = masks[0:NK, 4 * h + B * S // 2:4 * h + B * S // 2 + B * S // 4].bitcast(
            mybir.dt.uint8).rearrange("p (b s) -> p b s", b=B)
        crow = cut(work, 1536, [B, HK])
        cb = middle[0:1, 10112:10112 + 3 * HK // 2].bitcast(BF16).rearrange("p (n k) -> p n k", n=3)
        xng = [cut(work, 1024 * p, [4, D]) for p in range(2)]
        wq1s = cut(late, 0, [KD, D]); wk1s = cut(late, 512, [KD, D]); wv1s = cut(late, 1024, [KD, D])
        wo1s = cut(late, 1536, [KD, D])
        kb1 = cut(late, 2048, [B, 2, HALF])
        va = cut(late, 2048 + 2 * HK, [B, KC, 3, HD + 1])
        nets = 2048 + 2 * 2 * HALF * B // 2 + B * KC * 3 * (HD + 1)
        fw1 = cut(late, nets, [KD, 256]); fw2 = cut(late, nets + 512, [KD, P]); fw3 = cut(late, nets + 768, [64])
        fw4 = late[0:64, nets + 832:nets + 960]
        gwt1 = cut(late, nets + 960, [KD, P]); gwt2 = cut(late, nets + 1216, [64])
        gwt3 = late[0:64, nets + 1280:nets + 1408]
        sw13 = cut(late, 0, [2, KD, F]); sw2 = cut(late, 2048, [FC, D]); xT = cut(late, 3072, [NG, KD, G4])
        sil_s = cut(work, 0, [G4]); hs = cut(work, 512, [FC, G4])
        xg = [cut(work, 2560 + 256 * p, [D]) for p in range(2)]
        xgT = [cut(work, 3072 + 256 * p, [KD, P]) for p in range(2)]
        sil = [cut(work, 3584 + 512 * p, [F]) for p in range(2)]
        hh = [cut(work, 4608 + 512 * p, [F]) for p in range(2)]
        hT = [cut(work, 5632 + 512 * p, [FC, P]) for p in range(2)]
        yo = [cut(work, 6656 + 256 * p, [D]) for p in range(2)]
        ga = [[cut(work, 2560 + 256 * (2 * r + k), [D]) for k in range(2)] for r in range(4)]
        wrs = sb("w_router", [KD, NE])
        lg, lg2, ra, oh0, oh1, esc, tot0, tot1, rank = [cut(masks, T * NE * n, [T, NE]) for n in range(9)]
        cmp_ = cut(masks, T * NE * 9, [NE, T]); scmp = cut(masks, T * NE * 10, [SLOTS, NE])
        oh, tot = [oh0, oh1], [tot0, tot1]
        m1 = sb("top1", T); m2 = sb("top2", T); r1 = sb("route_r", T)
        esum = sb("route_sum", T); ersum = sb("route_rsum", T)
        wt = [sb(f"route_w{k}", T) for k in range(2)]
        msk = sb("route_mask", [T, NE], BF16)
        cnt = sb("route_count", NE); ntl = sb("route_tiles", NE)
        bs = [sb(f"route_base{k}", NE) for k in range(2)]
        sexp = sb("slot_expert_f", SLOTS)
        sei = sb("slot_expert", SLOTS, I32)
        pos = sb("row_f", T)
        idx = [sb(f"row_index{k}", T, U32) for k in range(2)]
        zero = work[:, 7168:7424]
        rows_in = nc.dram_tensor("expert_rows", (SLOTS * P, D), F32, kind="Internal").ap()
        rows_out = nc.dram_tensor("expert_outs", (SLOTS * P, D), F32, kind="Internal").ap()

        names = """ld_x ld_par ld_ctx ld_k ld_q ld_v ld_o ld_mask ld_bo ld_ffn ld_l1 ld_crow ld_w13 ld_w2 ld_sh
        dve_seq act_seq pool_seq var_done rstd_done memset_done gate_done
        su_mm su_kv su_crow su_g_mm su_g su_v_mm su_v bo_done ones_done su1_mm su1_dve su1_tm su1_t mask_done
        n_xn n_tx n_xt n_sc n_sub n_exp n_p n_tp n_pt n_pv n_res
        f_xn f_tx f_ev f_gcx f_gmm f_gact f_cpl f_l1 f_l2 f_l3 f_l4 f_a1 f_a2 f_a3 f_a4 f_upd f_bt f_res
        a_xn a_tx a_xt a_qm a_q a_sc a_sub a_exp a_tp a_pt a_pv a_att a_at a_atT a_wo a_res
        r_xn r_tx r_ev r_lg r_lgc r_e r_mask r_cnt r_pos r_zero r_scat
        s_h s_sil s_hs s_y s_res e_ld0 e_ld1 e_tx e_xt e_h e_sil e_hh e_th e_hTa e_hTv e_y e_yc e_st0 e_st1 c_ga0 c_ga1 c_ga2 c_ga3 c_use st_out""".split()
        q = {n: sem(n) for n in names}

        def tile_of(i, k):
            return i + k // 2 + (k % 2) * TB

        block = st.enter_context(nc.Block())

        @block.sync
        def _(sp):
            for n in range(4):
                sp.dma_start(xs[:, 4 * n:4 * n + 4, :],
                             x[512 * n:512 * n + 512, :].rearrange("(t p) d -> p t d", p=P)).then_inc(q["ld_x"], 16)
            sp.dma_start(ctx[:], ctxT).then_inc(q["ld_ctx"], 16)
            sp.dma_start(wk_s, wk0.rearrange("(k p) n -> p k n", p=P)).then_inc(q["ld_k"], 16)
            sp.dma_start(wv_s, wv0.rearrange("(k p) n -> p k n", p=P)).then_inc(q["ld_v"], 16)
            sp.dma_start(wq_s, wq0T.rearrange("(j p) n -> p j n", p=P)).then_inc(q["ld_q"], 16)
            sp.dma_start(wo_s, wo0.rearrange("(j p) n -> p j n", p=P)).then_inc(q["ld_o"], 16)
            for dst, src in ((wk1s, wk1), (wv1s, wv1), (wq1s, wq1), (wo1s, wo1)):
                sp.dma_start(dst, src.rearrange("(k p) n -> p k n", p=P)).then_inc(q["ld_l1"], 16)
            for dst, src in ((fw1[:], cw1.rearrange("(k p) n -> p k n", p=P)),
                             (fw2[:], cw2.rearrange("(k p) n -> p k n", p=P)), (fw3[:], cw3), (fw4[:], cw4),
                             (gwt1[:], gw1.rearrange("(k p) n -> p k n", p=P)), (gwt2[:], gw2), (gwt3[:], gw3),
                             (wrs[:], wr.rearrange("(k p) n -> p k n", p=P))):
                sp.dma_start(dst, src).then_inc(q["ld_ffn"], 16)
            for b in range(B):
                sp.wait_ge(q["su_crow"], b + 1)
                for n in range(3):
                    sp.dma_start(mrhs[b][NK + n:NK + n + 1, :], cb[:, n, :]).then_inc(q["ld_crow"], 16)
                sp.wait_ge(q["ld_crow"], 48 * (b + 1))
            sp.wait_ge(q["su_v"], B * KC // 2)
            for b in range(B):
                sp.dma_start(vo[BO_ROW:BO_ROW + 1, b, KC - 1, :], bo0).then_inc(q["ld_bo"], 16)
            sp.wait_ge(q["su1_t"], B * KC)
            for e in range(NE):
                sp.dma_start(w13[:, e, 0, :, :], w1[e].rearrange("(k p) n -> p k n", p=P)).then_inc(q["ld_w13"], 16)
                sp.dma_start(w13[:, e, 1, :, :], w3[e].rearrange("(k p) n -> p k n", p=P)).then_inc(q["ld_w13"], 16)
            sp.wait_ge(q["memset_done"], 1)
            for s in range(SLOTS):
                sp.dma_start(rows_in[s * P:(s + 1) * P, :], zero).then_inc(q["r_zero"], 16)
            sp.wait_ge(q["f_res"], T // 2)
            for e in range(NE):
                sp.dma_start(w2s[:, e, :, :], w2[e].rearrange("(f p) d -> p f d", p=P)).then_inc(q["ld_w2"], 16)
            sp.wait_ge(q["a_wo"], T)
            sp.dma_start(sw13[:, 0, :, :], ws1.rearrange("(k p) n -> p k n", p=P)).then_inc(q["ld_sh"], 16)
            sp.dma_start(sw13[:, 1, :, :], ws3.rearrange("(k p) n -> p k n", p=P)).then_inc(q["ld_sh"], 16)
            sp.dma_start(sw2, ws2.rearrange("(f p) d -> p f d", p=P)).then_inc(q["ld_sh"], 16)

            sp.wait_ge(q["r_scat"], 2 * T * 16)

            def load(i, k):
                s = 2 * i + k
                after(sp, q["e_tx"], s - 1)
                sp.dma_start(xg[k], rows_in[bass.ds(s * P, P), :]).then_inc(q[f"e_ld{k}"], 16)

            def store(i, k):
                s = 2 * i + k
                sp.wait_ge(q["e_yc"], s + 1)
                sp.dma_start(rows_out[bass.ds(s * P, P), :], yo[k]).then_inc(q[f"e_st{k}"], 16)

            load(0, 0)
            load(0, 1)
            with sp.Fori(1, SLOTS // 2) as i:
                for k in range(2):
                    load(i, k)
                    store(i - 1, k)
            load(SLOTS // 2, 0)
            for s in range(SLOTS - 3, SLOTS):
                store(s // 2, s % 2)
            for t in range(0, T, 4):
                sp.wait_ge(q["c_use"], t + 4)
                sp.wait_ge(q["s_res"], t // 2 + 3)
                sp.dma_start(out[t * P:(t + 4) * P, :].rearrange("(t p) d -> p t d", p=P),
                             xs[:, t:t + 4, :]).then_inc(q["st_out"], 16)
            sp.wait_ge(q["st_out"], 64)

        @block.gpsimd
        def _(pool):
            pool.dma_start(con[:], consts).then_inc(q["ld_par"], 16)
            pool.dma_start(par[:], small).then_inc(q["ld_par"], 16)
            pool.dma_start(mask_u8[:], maskT).then_inc(q["ld_mask"], 16)
            pool.dma_start(mrow_u8[:], mask1).then_inc(q["ld_mask"], 16)
            nc.gpsimd.memset(mhalf[:], -0.5).then_inc(q["pool_seq"], 1)
            pool.wait_ge(q["pool_seq"], 1)
            for n in range(4):
                pool.wait_ge(q["var_done"], n + 1)
                nc.gpsimd.tensor_tensor(rstd[:], vare[:], mhalf[:], ALU.pow).then_inc(q["rstd_done"], 1)
            pool.wait_ge(q["r_zero"], 16 * SLOTS)
            pool.wait_ge(q["r_pos"], 2)
            for t in range(T):
                for k in range(2):
                    pool.indirect_dma_start(rows_in[:, :], bass.IndirectOffsetOnAxis(ap=idx[k][:, t:t + 1], axis=0),
                                            xn4[:, t, :], None).then_inc(q["r_scat"], 16)
            pool.wait_ge(q["e_st0"], 16 * ((SLOTS + 1) // 2))
            pool.wait_ge(q["e_st1"], 16 * (SLOTS // 2))
            for t in range(T):
                after(pool, q["c_use"], t - 3)
                for k in range(2):
                    pool.indirect_dma_start(ga[t % 4][k], None, rows_out[:, :],
                                            bass.IndirectOffsetOnAxis(ap=idx[k][:, t:t + 1], axis=0)
                                            ).then_inc(q[f"c_ga{t % 4}"], 16)

        @block.tensor
        def _(pe):
            def mm(o, l, r, start=True, stop=True, **kw):
                return nc.tensor.matmul(o, l, r, start=start, stop=stop, **kw)

            def tr(o, i, rows=P):
                return nc.tensor.transpose(o, i, ident[0:rows, 0:rows])

            pe.wait_ge(q["ld_ctx"], 16)
            for w, (ws, ready) in enumerate(((wk_s, "ld_k"), (wv_s, "ld_v"))):
                pe.wait_ge(q[ready], 16)
                for u in range(3):
                    for j in range(3 * u, min(3 * u + 3, PAIRS)):
                        o = ps[:, 3 * w + u, PW * (j - 3 * u):PW * (j - 3 * u) + PW]
                        for k in range(KD):
                            last = mm(o, ws[:, k, P * j:P * j + P], ctx[:, k, :], k == 0, k == KD - 1)
                    last.then_inc(q["su_mm"], 1)
            pe.wait_ge(q["ld_q"], 16)
            pe.wait_ge(q["ld_par"], 32)
            pe.wait_ge(q["su_kv"], 6)
            for b in range(B):
                if b:
                    pe.wait_ge(q["su_crow"], 1)
                for u in range(3):
                    for j in range(3 * u, min(3 * u + 3, PAIRS)):
                        o = ps[0:1, u, PW * (j - 3 * u):PW * (j - 3 * u) + PW]
                        last = mm(o, par[:, V_BQ + j:V_BQ + j + 1], kbd[:, b, j, :])
                    last.then_inc(q["su_mm"], 1)
                for m in range(KD):
                    for u in range(3):
                        n = 6 * b + 3 * m + u
                        after(pe, q["su_g"], n - 4)
                        for j in range(3 * u, min(3 * u + 3, PAIRS)):
                            o = ps[:, 3 + n % 5, PW * (j - 3 * u):PW * (j - 3 * u) + PW]
                            last = mm(o, wq_s[:, j, P * m:P * m + P], kbd[:, b, j, :])
                        last.then_inc(q["su_g_mm"], 1)
            pe.wait_ge(q["ld_o"], 16)
            pe.wait_ge(q["su_g"], 12)
            for b in range(B):
                for n in range(KC // 2):
                    m = b * (KC // 2) + n
                    after(pe, q["su_v"], m - 4)
                    for c in (2 * n, 2 * n + 1):
                        js = range(c * P // PW, (min(c * P + P, HK) - 1) // PW + 1)
                        for j in js:
                            at = P + ZS * j + c * P - PW * j
                            last = mm(ps[:, 3 + m % 5, D * (c % 2):D * (c % 2) + D], zv[:, b, at:at + P],
                                      wo_s[:, j, :], j == js[0], j == js[-1])
                    last.then_inc(q["su_v_mm"], 1)
            pe.wait_ge(q["ld_l1"], 64)
            pe.wait_ge(q["su_crow"], 2)
            for w, ws in enumerate((wk1s, wv1s)):
                for m in range(2):
                    for k in range(KD):
                        last = mm(ps[:, w, PW * m:PW * m + PW], ws[:, k, P * m:P * m + P], ctx[:, k, :],
                                  k == 0, k == KD - 1)
                last.then_inc(q["su1_mm"], 1)
            pe.wait_ge(q["su1_dve"], 2)
            for b in range(B):
                for c in range(KC):
                    n = KC * b + c
                    after(pe, q["su1_t"], n - 1)
                    for m in halves_of(c):
                        at = ZL + c * P - HALF * m
                        last = tr(ps[:, 1 + n % 2, P * m:P * m + P], z1[:, b, m, at:at + P])
                    last.then_inc(q["su1_tm"], 1)

            def xt(i, k, pre):
                t = 2 * i + k
                pe.wait_ge(q[pre + "_xn"], t + 1)
                after(pe, q["n_xt" if pre == "n" else "a_q"], t)
                for m in range(KD):
                    last = tr(ps[:, 5, P * m:P * m + P], xn[k % 2][:, P * m:P * m + P])
                last.then_inc(q[pre + "_tx"], 1)

            def trans_p(i, k, pre, ready):
                t = 2 * i + k
                pe.wait_ge(q[pre + ready], t + 1)
                for j, (c0, c1) in enumerate(PTG):
                    after(pe, q[pre + "_pt"], 3 * t + j - 1)
                    for c in range(c0, c1):
                        w = min(P, HK - P * c)
                        last = tr(ps[0:w, 3 + (k + j) % 2, P * (c - c0):P * (c - c0) + P],
                                  sc[k % 2][:, P * c:P * c + w])
                    last.then_inc(q[pre + "_tp"], 1)

            def scores0(i, k):
                t = 2 * i + k
                p = k % 2
                pe.wait_ge(q["n_xt"], t + 1)
                for u, (a, z) in enumerate(UNITS):
                    after(pe, q["n_sub"], 3 * t - 2 + u)
                    n = NK * (z - a)
                    for m in range(KD):
                        mm(ps[:, u, 0:n], xnT[p][:, m, :], gk[:, p, m, NK * a:NK * z], m == 0, False)
                    mm(ps[:, u, 0:n], mlhs[:, p, bass.ds((i + k // 2) * P, P)], mrhs[p][:, NK * a:NK * z],
                       False, True).then_inc(q["n_sc"], 1)

            def pv0(i, k):
                t = 2 * i + k
                p = k % 2
                after(pe, q["n_res"], t - 1)
                for c in range(KC):
                    if c % 4 == 0:
                        pe.wait_ge(q["n_pt"], 3 * t + c // 4 + 1)
                    last = mm(ps[:, 6 + p, 0:D], pt[p][:, c, :], vo[:, p, c, :], c == 0, c == KC - 1)
                last.then_inc(q["n_pv"], 1)

            def step0(i, k, prev=True, nxt=True):
                scores0(i, k)
                if prev:
                    trans_p(i, k - 1, "n", "_p")
                if nxt:
                    xt(i, k + 1, "n")
                if prev:
                    pv0(i, k - 1)

            pe.wait_ge(q["su_v"], B * KC // 2)
            pe.wait_ge(q["bo_done"], 1)
            pe.wait_ge(q["ld_crow"], 48 * B)
            pe.wait_ge(q["mask_done"], 1)
            pe.wait_ge(q["su1_t"], B * KC)
            xt(0, 0, "n")
            step0(0, 0, prev=False)
            step0(0, 1)
            with pe.Fori(1, TB - 1) as i:
                step0(i, 0)
                step0(i, 1)
            step0(TB - 1, 0)
            step0(TB - 1, 1, nxt=False)
            trans_p(TB - 1, 1, "n", "_p")
            pv0(TB - 1, 1)

            pe.wait_ge(q["n_res"], T)
            for g in range(NG):
                pe.wait_ge(q["f_xn"], 4 * g + 4)
                for m in range(KD):
                    for j in range(4):
                        last = tr(ps[:, 2 * g + m, P * j:P * j + P], xng[g % 2][:, j, P * m:P * m + P])
                    last.then_inc(q["f_tx"], 1)
            pe.wait_ge(q["ld_ffn"], 128)
            pe.wait_ge(q["f_gcx"], 1)
            for m in range(KD):
                last = mm(ps[:, 7, 0:B], gwt1[:, m, :], gcx[:, m, :], m == 0, m == KD - 1)
            last.then_inc(q["f_gmm"], 1)
            pe.wait_ge(q["f_gact"], 1)
            mm(ps[0:64, 7, 0:B], gwt2[:], gh1[:]).then_inc(q["f_gmm"], 1)
            pe.wait_ge(q["f_gact"], 2)
            mm(ps[:, 7, 0:B], gwt3[:], gh2[:]).then_inc(q["f_gmm"], 1)
            pe.wait_ge(q["f_a4"], 1)

            with pe.Fori(0, 3) as c:
                for pair in range(NG // 2):
                    gs = (2 * pair, 2 * pair + 1)
                    for g in gs:
                        n = 4 * c + g
                        pe.wait_ge(q["f_upd"], n + 1)
                        for o in range(2):
                            for m in range(KD):
                                last = mm(ps[:, 4 * (g % 2) + o, :], fw1[:, m, P * o:P * o + P], st_x[:, m, g, :],
                                          m == 0, m == KD - 1)
                            last.then_inc(q["f_l1"], 1)
                    for g in gs:
                        n = 4 * c + g
                        pe.wait_ge(q["f_a1"], 2 * n + 2)
                        pe.wait_ge(q["f_upd"], n + 3)
                        for m in range(KD):
                            last = mm(ps[:, 4 * (g % 2) + 2, :], fw2[:, m, :], h1[g % 2][:, m, :],
                                      m == 0, m == KD - 1)
                        last.then_inc(q["f_l2"], 1)
                    for g in gs:
                        n = 4 * c + g
                        pe.wait_ge(q["f_a2"], n + 1)
                        mm(ps[0:64, 4 * (g % 2) + 3, :], fw3[:], h2[g % 2]).then_inc(q["f_l3"], 1)
                    for g in gs:
                        n = 4 * c + g
                        pe.wait_ge(q["f_a3"], n + 1)
                        mm(ps[:, 4 * (g % 2) + 2, :], fw4[:], h3[g % 2][0:64, :]).then_inc(q["f_l4"], 1)
            pe.wait_ge(q["f_a4"], 3 * NG + 1)
            for n in range(T // 2):
                g = n // 2
                pe.wait_ge(q["f_upd"], 3 * NG + g + 1)
                for j in range(2):
                    for m in range(KD):
                        at = P * (2 * (n % 2) + j)
                        last = tr(ps[:, n, D * j + P * m:D * j + P * m + P], st_x[:, m, g, at:at + P])
                last.then_inc(q["f_bt"], 1)

            def queries(i, k):
                t = 2 * i + k
                pe.wait_ge(q["a_xt"], t + 1)
                for o in range(2):
                    for m in range(KD):
                        last = mm(ps[:, 5, P * o:P * o + P], wq1s[:, m, P * o:P * o + P], xnT[k % 2][:, m, :],
                                  m == 0, m == KD - 1)
                last.then_inc(q["a_qm"], 1)

            def scores1(i, k):
                t = 2 * i + k
                p = k % 2
                pe.wait_ge(q["a_q"], t + 1)
                for u, (a, z) in enumerate(UNITS):
                    after(pe, q["a_sub"], 3 * t - 2 + u)
                    c0, c1 = NK * a, NK * z
                    mm(ps[:, u, 0:c1 - c0], ones_bf[0:1, :], mrow[p][:, c0:c1], True, True)
                    parts = [(m, max(c0, HALF * m), min(c1, HALF * (m + 1))) for m in range(2)]
                    parts = [x for x in parts if x[1] < x[2]]
                    for m, x0, x1 in parts:
                        last = mm(ps[:, u, x0 - c0:x1 - c0], qT[p][:, m, :], kb1[:, p, m, x0 - HALF * m:x1 - HALF * m],
                                  False, True, skip_group_check=True)
                    last.then_inc(q["a_sc"], 1)

            def pv1(i, k):
                t = 2 * i + k
                p = k % 2
                after(pe, q["a_att"], t)
                for c in range(KC):
                    if c % 4 == 0:
                        pe.wait_ge(q["a_pt"], 3 * t + c // 4 + 1)
                    h0, n = heads_of(c)
                    last = mm(ps[:, 6, 17 * h0:17 * (h0 + n)], pt[p][:, c, :], va[:, p, c, 0:n, :],
                              c == 0, True, skip_group_check=True)
                last.then_inc(q["a_pv"], 1)

            def att_t(i, k):
                t = 2 * i + k
                pe.wait_ge(q["a_att"], t + 1)
                after(pe, q["a_res"], t)
                for m in range(KD):
                    last = tr(ps[:, 7, P * m:P * m + P], att[:, P * m:P * m + P])
                last.then_inc(q["a_at"], 1)

            def out1(i, k):
                t = 2 * i + k
                pe.wait_ge(q["a_atT"], t + 1)
                for m in range(KD):
                    last = mm(ps[:, 7, 0:D], attT[:, m, :], wo1s[:, m, :], m == 0, m == KD - 1)
                last.then_inc(q["a_wo"], 1)

            def step1(i, k, p1=True, p2=True, nxt=True):
                scores1(i, k)
                if p2:
                    att_t(i, k - 2)
                if p1:
                    trans_p(i, k - 1, "a", "_exp")
                if p2:
                    out1(i, k - 2)
                if nxt:
                    xt(i, k + 1, "a")
                if p1:
                    pv1(i, k - 1)
                if nxt:
                    queries(i, k + 1)

            pe.wait_ge(q["f_res"], T // 2)
            xt(0, 0, "a")
            queries(0, 0)
            step1(0, 0, p1=False, p2=False)
            step1(0, 1, p2=False)
            step1(1, 0)
            step1(1, 1)
            with pe.Fori(2, TB - 1) as i:
                step1(i, 0)
                step1(i, 1)
            step1(TB - 1, 0)
            step1(TB - 1, 1, nxt=False)
            att_t(TB - 1, 0)
            trans_p(TB - 1, 1, "a", "_exp")
            out1(TB - 1, 0)
            pv1(TB - 1, 1)
            att_t(TB - 1, 1)
            out1(TB - 1, 1)

            for g in range(NG):
                pe.wait_ge(q["r_xn"], 4 * g + 4)
                if g == 0:
                    pe.wait_ge(q["a_res"], T)
                after(pe, q["r_ev"], 2 * g - 2)
                for m in range(KD):
                    for j in range(4):
                        last = tr(ps[:, 2 * (g % 2) + m, P * j:P * j + P], xn4[:, 4 * g + j, P * m:P * m + P])
                    last.then_inc(q["r_tx"], 1)
                pe.wait_ge(q["r_ev"], 2 * g + 2)
                for j in range(4):
                    for m in range(KD):
                        last = mm(ps[:, 4 + g, NE * j:NE * j + NE], xT[:, g, m, P * j:P * j + P], wrs[:, m, :],
                                  m == 0, m == KD - 1)
                last.then_inc(q["r_lg"], 1)
            pe.wait_ge(q["r_lgc"], NG)
            pe.wait_ge(q["r_mask"], 1)
            rhs = msk[:].rearrange("p t e -> p (t e)")
            mm(ps[:, 6, 0:T * NE], up_bf[:], rhs).then_inc(q["s_y"], 1)
            mm(ps[:, 7, 0:T * NE], ones_bf[:], rhs).then_inc(q["r_e"], 1)

            def shared(g0, g1):
                with pe.Fori(g0, g1) as g:
                    for f in range(FC):
                        n = 4 * g + f
                        if f >= 2:
                            pe.wait_ge(q["s_hs"], n)
                        for w in range(2):
                            for m in range(KD):
                                last = mm(ps[:, 2 * (f % 2) + w, :], sw13[:, w, m, P * f:P * f + P],
                                          xT[:, g, m, :], m == 0, m == KD - 1)
                            last.then_inc(q["s_h"], 1)
                    pe.wait_ge(q["s_hs"], 4 * g + 5)
                    pe.wait_ge(q["s_res"], 2 * g + 1)
                    for u in range(2):
                        for j in range(2):
                            for f in range(FC):
                                at = P * (2 * u + j)
                                last = mm(ps[:, 4 + u, D * j:D * j + D], hs[:, f, at:at + P], sw2[:, f, :],
                                          f == 0, f == FC - 1)
                        last.then_inc(q["s_y"], 1)

            pe.wait_ge(q["ld_sh"], 48)
            shared(0, NG // 2)

            expert = [None, None]

            def e_trans(i, k):
                s = 2 * i + k
                pe.wait_ge(q[f"e_ld{k % 2}"], 16 * (i + k // 2 + 1))
                after(pe, q["e_xt"], s)
                for m in range(KD):
                    last = tr(ps[:, 4, P * m:P * m + P], xg[k % 2][:, P * m:P * m + P])
                last.then_inc(q["e_tx"], 1)

            def e_up(i, k):
                s = 2 * i + k
                p = k % 2
                pe.wait_ge(q["e_xt"], s + 1)
                after(pe, q["e_hh"], s - 1)
                e = pe.value_load(sei[0:1, bass.ds(s, 1)], min_val=0, max_val=NE - 1)
                for w in range(2):
                    for m in range(KD):
                        last = mm(ps[:, 2 * p + w, :], xgT[p][:, m, :],
                                  w13[:, bass.ds(e, 1), w, m, :].rearrange("p a n -> p (a n)"), m == 0, m == KD - 1)
                    last.then_inc(q["e_h"], 1)

            def e_hidden_t(i, k):
                s = 2 * i + k
                pe.wait_ge(q["e_hh"], s + 1)
                after(pe, q["e_hTa"], s)
                after(pe, q["e_hTv"], s)
                for u in range(2):
                    for f in range(2):
                        last = tr(ps[:, 5 + u, P * f:P * f + P], hh[k % 2][:, P * (2 * u + f):P * (2 * u + f) + P])
                    last.then_inc(q["e_th"], 1)

            def e_down(i, k):
                s = 2 * i + k
                e = pe.value_load(sei[0:1, bass.ds(s, 1)], min_val=0, max_val=NE - 1)
                pe.wait_ge(q["e_hTa"], s + 1)
                pe.wait_ge(q["e_hTv"], s + 1)
                after(pe, q["e_yc"], s)
                for f in range(FC):
                    last = mm(ps[:, 7, 0:D], hT[k % 2][:, f, :],
                              w2s[:, bass.ds(e, 1), f, :].rearrange("p a n -> p (a n)"), f == 0, f == FC - 1)
                last.then_inc(q["e_y"], 1)

            def e_step(i, k, prev=True, nxt=True):
                e_up(i, k)
                if prev:
                    e_hidden_t(i, k - 1)
                if nxt:
                    e_trans(i, k + 1)
                if prev:
                    e_down(i, k - 1)

            pe.wait_ge(q["ld_w13"], 32 * NE)
            pe.wait_ge(q["ld_w2"], 16 * NE)
            pe.wait_ge(q["s_res"], NG + 1)
            e_trans(0, 0)
            e_step(0, 0, prev=False)
            e_step(0, 1)
            e_step(1, 0)
            e_step(1, 1)
            with pe.Fori(2, SLOTS // 2) as i:
                e_step(i, 0)
                e_step(i, 1)
            e_step(SLOTS // 2, 0, nxt=False)
            e_hidden_t(SLOTS // 2, 0)
            e_down(SLOTS // 2, 0)
            pe.wait_ge(q["e_yc"], SLOTS)
            shared(NG // 2, NG)

        @block.scalar
        def _(act):
            def copy(o, i):
                return nc.scalar.activation(o, i, ACT.Copy)

            act.wait_ge(q["ld_par"], 32)
            nc.scalar.activation(gate[:], par[:, V_GX:V_GX + 4], ACT.Tanh).then_inc(q["gate_done"], 1)
            for n in range(12):
                b, m, u = n // 6, n // 3 % 2, n % 3
                a, z = UNITS[u]
                act.wait_ge(q["su_g_mm"], n + 1)
                copy(gk[:, b, m, NK * a:NK * z], ps[:, 3 + n % 5, 0:NK * (z - a)]).then_inc(q["su_g"], 1)
            act.wait_ge(q["gate_done"], 1)
            for n in range(B * KC // 2):
                b, c = n // (KC // 2), 2 * (n % (KC // 2))
                act.wait_ge(q["su_v_mm"], n + 1)
                nc.scalar.activation(vo[:, b, c:c + 2, :].rearrange("p c d -> p (c d)"), ps[:, 3 + n % 5, :],
                                     ACT.Copy, scale=gate[:, 0:1]).then_inc(q["su_v"], 1)
            act.wait_ge(q["ones_done"], B)
            for n in range(B * KC):
                b, c = n // KC, n % KC
                h0, nh = heads_of(c)
                act.wait_ge(q["su1_tm"], n + 1)
                for m in halves_of(c):
                    a, z = max(h0, 8 * m), min(h0 + nh, 8 * m + 8)
                    src = ps[:, 1 + n % 2, P * m + HD * (a - 8 * m):P * m + HD * (z - 8 * m)]
                    last = copy(va[:, b, c, a - h0:z - h0, 0:HD], src.rearrange("p (h d) -> p h d", d=HD))
                last.then_inc(q["su1_t"], 1)

            def ev_xt(i, k, pre, used):
                t = 2 * i + k
                act.wait_ge(q[pre + "_tx"], t + 1)
                if used == "n_sc":
                    after(act, q["n_sc"], 3 * t - 3)
                else:
                    after(act, q["a_qm"], t - 1)
                copy(xnT[k % 2].rearrange("p k t -> p (k t)"), ps[:, 5, 0:D]).then_inc(q[pre + "_xt"], 1)

            def ev_pt(i, k, pre):
                t = 2 * i + k
                after(act, q[pre + "_pv"], t - 1)
                for j, (c0, c1) in enumerate(PTG):
                    act.wait_ge(q[pre + "_tp"], 3 * t + j + 1)
                    bank = ps[:, 3 + (k + j) % 2, :]
                    if c1 < KC:
                        last = copy(pt[k % 2][:, c0:c1, :].rearrange("p c t -> p (c t)"), bank[:, 0:P * (c1 - c0)])
                    else:
                        copy(pt[k % 2][:, c0, :], bank[:, 0:P])
                        last = copy(pt[k % 2][0:LASTK, c0 + 1, :], bank[0:LASTK, P:2 * P])
                    last.then_inc(q[pre + "_pt"], 1)

            def exps(i, k, pre, scale):
                t = 2 * i + k
                act.wait_ge(q[pre + "_sub"], 3 * t + 3)
                nc.scalar.activation(sc[k % 2], sc[k % 2], ACT.Exp, scale=scale).then_inc(q[pre + "_exp"], 1)

            def step0(i, k, prev=True, nxt=True):
                if prev:
                    ev_pt(i, k - 1, "n")
                if nxt:
                    ev_xt(i, k + 1, "n", "n_sc")
                exps(i, k, "n", DK ** -0.5)

            ev_xt(0, 0, "n", "n_sc")
            step0(0, 0, prev=False)
            step0(0, 1)
            with act.Fori(1, TB - 1) as i:
                step0(i, 0)
                step0(i, 1)
            step0(TB - 1, 0)
            step0(TB - 1, 1, nxt=False)
            ev_pt(TB - 1, 1, "n")

            for g in range(NG):
                for m in range(KD):
                    act.wait_ge(q["f_tx"], 2 * g + m + 1)
                    last = nc.scalar.activation(st_x[:, m, g, :], ps[:, 2 * g + m, :], ACT.Copy,
                                                accum_out=csum[:, m, g:g + 1])
                last.then_inc(q["f_upd"], 1)
            act.wait_ge(q["f_gmm"], 1)
            nc.scalar.activation(gh1[:], ps[:, 7, 0:B], ACT.Gelu, bias=par[:, V_GB1:V_GB1 + 1]).then_inc(q["f_gact"], 1)
            act.wait_ge(q["f_gmm"], 2)
            nc.scalar.activation(gh2[:], ps[0:64, 7, 0:B], ACT.Gelu,
                                 bias=par[0:64, V_GB2:V_GB2 + 1]).then_inc(q["f_gact"], 1)
            act.wait_ge(q["f_gmm"], 3)
            act.wait_ge(q["f_cpl"], 1)
            nc.scalar.activation(gtan[:], ps[:, 7, 0:B], ACT.Tanh, bias=hb[:, 0:1], scale=0.5).then_inc(q["f_a4"], 1)
            with act.Fori(0, 3) as c:
                for pair in range(NG // 2):
                    gs = (2 * pair, 2 * pair + 1)
                    for g in gs:
                        n = 4 * c + g
                        for o in range(2):
                            act.wait_ge(q["f_l1"], 2 * n + o + 1)
                            nc.scalar.activation(h1[g % 2][:, o, :], ps[:, 4 * (g % 2) + o, :], ACT.Gelu,
                                                 bias=par[:, V_CB1 + o:V_CB1 + o + 1]).then_inc(q["f_a1"], 1)
                    for g in gs:
                        n = 4 * c + g
                        act.wait_ge(q["f_l2"], n + 1)
                        nc.scalar.activation(h2[g % 2], ps[:, 4 * (g % 2) + 2, :], ACT.Gelu,
                                             bias=par[:, V_CB2:V_CB2 + 1]).then_inc(q["f_a2"], 1)
                    for g in gs:
                        n = 4 * c + g
                        act.wait_ge(q["f_l3"], n + 1)
                        nc.scalar.activation(h3[g % 2][0:64, :], ps[0:64, 4 * (g % 2) + 3, :], ACT.Gelu,
                                             bias=par[0:64, V_CB3:V_CB3 + 1]).then_inc(q["f_a3"], 1)
                    for g in gs:
                        n = 4 * c + g
                        act.wait_ge(q["f_l4"], n + 1)
                        act.wait_ge(q["f_upd"], n + 3)
                        nc.scalar.activation(tt[g % 2], ps[:, 4 * (g % 2) + 2, :], ACT.Tanh, bias=hb[:, 1:2],
                                             scale=0.5).then_inc(q["f_a4"], 1)

            def ev_at(i, k):
                t = 2 * i + k
                act.wait_ge(q["a_at"], t + 1)
                after(act, q["a_wo"], t)
                copy(attT.rearrange("p k t -> p (k t)"), ps[:, 7, 0:D]).then_inc(q["a_atT"], 1)

            def ev_q(i, k):
                t = 2 * i + k
                act.wait_ge(q["a_qm"], t + 1)
                after(act, q["a_sc"], 3 * t - 3)
                copy(qT[k % 2].rearrange("p k t -> p (k t)"), ps[:, 5, 0:D]).then_inc(q["a_q"], 1)

            def step1(i, k, p1=True, p2=True, nxt=True):
                if p2:
                    ev_at(i, k - 2)
                if p1:
                    ev_pt(i, k - 1, "a")
                if nxt:
                    ev_xt(i, k + 1, "a", "a_qm")
                exps(i, k, "a", HD ** -0.5)
                if nxt:
                    ev_q(i, k + 1)

            ev_xt(0, 0, "a", "a_qm")
            ev_q(0, 0)
            step1(0, 0, p1=False, p2=False)
            step1(0, 1, p2=False)
            step1(1, 0)
            step1(1, 1)
            with act.Fori(2, TB - 1) as i:
                step1(i, 0)
                step1(i, 1)
            step1(TB - 1, 0)
            step1(TB - 1, 1, nxt=False)
            ev_at(TB - 1, 0)
            ev_pt(TB - 1, 1, "a")
            ev_at(TB - 1, 1)

            for n in range(2 * NG):
                g, m = n // 2, n % 2
                act.wait_ge(q["r_tx"], n + 1)
                copy(xT[:, g, m, :], ps[:, 2 * (g % 2) + m, :]).then_inc(q["r_ev"], 1)
            act.wait_ge(q["r_lgc"], NG + 1)
            nc.scalar.activation(esc[:], esc[:], ACT.Exp).then_inc(q["r_e"], 1)

            def shared(g0, g1):
                with act.Fori(g0, g1) as g:
                    for f in range(FC):
                        n = 4 * g + f
                        act.wait_ge(q["s_h"], 2 * n + 1)
                        act.wait_ge(q["s_hs"], n + 1)
                        nc.scalar.activation(sil_s, ps[:, 2 * (f % 2), :], ACT.Silu).then_inc(q["s_sil"], 1)

            def e_xt(i, k):
                s = 2 * i + k
                act.wait_ge(q["e_tx"], s + 1)
                after(act, q["e_h"], 2 * (s - 1))
                copy(xgT[k % 2].rearrange("p k t -> p (k t)"), ps[:, 4, 0:D]).then_inc(q["e_xt"], 1)

            def e_ht(i, k):
                s = 2 * i + k
                act.wait_ge(q["e_th"], 2 * s + 1)
                after(act, q["e_y"], s - 1)
                copy(hT[k % 2][:, 0:2, :].rearrange("p f t -> p (f t)"), ps[:, 5, 0:2 * P]).then_inc(q["e_hTa"], 1)

            def e_silu(i, k):
                s = 2 * i + k
                act.wait_ge(q["e_h"], 2 * s + 1)
                after(act, q["e_hh"], s - 1)
                nc.scalar.activation(sil[k % 2], ps[:, 2 * (k % 2), :], ACT.Silu).then_inc(q["e_sil"], 1)

            def e_step(i, k, prev=True, nxt=True):
                if prev:
                    e_ht(i, k - 1)
                if nxt:
                    e_xt(i, k + 1)
                e_silu(i, k)

            shared(0, NG // 2)
            e_xt(0, 0)
            e_step(0, 0, prev=False)
            e_step(0, 1)
            e_step(1, 0)
            e_step(1, 1)
            with act.Fori(2, SLOTS // 2) as i:
                e_step(i, 0)
                e_step(i, 1)
            e_step(SLOTS // 2, 0, nxt=False)
            e_ht(SLOTS // 2, 0)
            shared(NG // 2, NG)

        @block.vector
        def _(dve):
            v = nc.vector
            seq = Chain(dve, q["dve_seq"])

            def norm_stats(tile):
                seq.mark(v.bn_stats(stats[:, tile, :], xs[:, tile, :]))

            def norm(o, tile):
                return v.tensor_scalar(o, xs[:, tile, :], mv[:, tile, 0:1], rstd[:, tile:tile + 1]
                                       if isinstance(tile, int) else rstd[:, bass.ds(tile, 1)],
                                       ALU.subtract, ALU.mult)

            def variances(n):
                seq.sync()
                for t in range(T):
                    seq.mark(v.bn_aggr(mv[:, t, :], stats[:, t, :]))
                seq.sync()
                v.tensor_scalar(vare[:], mv[:, :, 1], EPS, None, ALU.add).then_inc(q["var_done"], 1)
                dve.wait_ge(q["rstd_done"], n)

            dve.wait_ge(q["ld_x"], 64)
            for t in range(T):
                seq.mark(v.bn_stats(stats[:, t, :], xs[:, t, :]))
            seq.sync()
            for t in range(T):
                seq.mark(v.bn_aggr(mv[:, t, :], stats[:, t, :]))
            seq.sync()
            v.tensor_scalar(vare[:], mv[:, :, 1], EPS, None, ALU.add).then_inc(q["var_done"], 1)
            v.memset(zero, 0.0).then_inc(q["memset_done"], 1)
            seq.mark(v.memset(kbd.rearrange("p b j n -> p (b j n)"), 0.0))
            seq.mark(v.memset(zv.rearrange("p b n -> p (b n)"), 0.0))
            seq.mark(v.memset(ones_bf[:], 1.0))
            seq.mark(v.memset(mlhs[:], 1.0))
            for p in range(2):
                seq.mark(v.memset(pt[p][:, KC - 1, :], 0.0))
            seq.sync()
            for p in range(2):
                last = v.memset(pt[p][BO_ROW:BO_ROW + 1, KC - 1, :], 1.0)
                seq.mark(last)
            dve.wait_ge(q["ld_par"], 32)
            seq.mark(v.tensor_copy(up_bf[:], con[:, C_UP:C_UP + P]))
            seq.mark(v.tensor_scalar(hb[:, 0:1], par[:, V_GB3:V_GB3 + 1], 0.5, None, ALU.mult))
            seq.mark(v.tensor_scalar(hb[:, 1:2], par[:, V_CB4:V_CB4 + 1], 0.5, None, ALU.mult))
            for b in range(B):
                v.tensor_copy(va[:, b, :, :, HD],
                              con[:, C_IN:C_IN + 3 * KC].rearrange("p (c h) -> p c h", h=3)).then_inc(q["ones_done"], 1)
            dve.wait_ge(q["ld_mask"], 32)
            seq.mark(v.tensor_scalar(mlhs[0:NK, :, :], mask_u8[:], BIG, -BIG, ALU.mult, ALU.add))
            for b in range(B):
                seq.mark(v.tensor_copy(mrhs[b][0:NK, :].rearrange("p (h t) -> p h t", h=H),
                                       spread(ident[0:NK, 0:NK], 1, [NK, H, NK])))
            seq(v.tensor_scalar(mrf[:], mrow_u8[:], BIG, -BIG, ALU.mult, ALU.add))
            seq(v.tensor_reduce(mval[:, 0:2], mrow_u8[:], AX.X, ALU.add))
            seq(v.reciprocal(mval[:, 2:4], mval[:, 0:2]))
            seq(v.tensor_scalar(mval[:, 0:2], mval[:, 2:4], 0.0, None, ALU.mult))
            for b in range(B):
                seq.mark(v.tensor_scalar(mrow[b][:].rearrange("p (h t) -> p h t", h=H),
                                         spread(mrf[:, b, :], 1, [1, H, NK]), mval[:, b:b + 1], None, ALU.add))
            seq.sync()
            v.memset(den[:], 0.0).then_inc(q["mask_done"], 1)

            for w, col in enumerate((V_BK, V_BV)):
                for u in range(3):
                    j0, j1 = 3 * u, min(3 * u + 3, PAIRS)
                    dve.wait_ge(q["su_mm"], 3 * w + u + 1)
                    for r in range(2):
                        rows = slice(64 * r, 64 * r + 64)
                        src = ps[rows, 3 * w + u, 0:PW * (j1 - j0)].rearrange("p (j b t) -> p j b t", b=B, t=NK)
                        for b in range(B):
                            if w == 0:
                                o = kbd[rows, b, j0:j1, NK * r:NK * r + NK]
                            else:
                                o = zv[rows, b, P:P + PAIRS * ZS].rearrange("p (j s) -> p j s", s=ZS)[
                                    :, j0:j1, NK * r:NK * r + NK]
                            last = v.tensor_tensor(o, src[:, :, b, :],
                                                   spread(par[rows, col + j0:col + j1], 2, [64, j1 - j0, NK]), ALU.add)
                    last.then_inc(q["su_kv"], 1)
            for b in range(B):
                dve.wait_ge(q["su_mm"], 6 + 3 * (b + 1))
                for u, (a, z) in enumerate(UNITS):
                    seq.mark(v.tensor_copy(crow[0:1, b, NK * a:NK * z], ps[0:1, u, 0:NK * (z - a)]))
                seq.sync()
                if b:
                    dve.wait_ge(q["ld_crow"], 48 * b)
                c = crow[0:1, b, :]
                for n in range(2):
                    seq(v.tensor_copy(cb[:, n, :], c))
                    seq(v.tensor_tensor(c, c, cb[:, n, :], ALU.subtract))
                v.tensor_copy(cb[:, 2, :], c).then_inc(q["su_crow"], 1)
            pads = [(0, ZL), (ZL + HALF, Z1)]
            for a, z in pads:
                seq.mark(v.memset(z1[:, :, :, a:z], 0.0))
            for w in range(2):
                dve.wait_ge(q["su1_mm"], w + 1)
                src = ps[:, w, 0:2 * PW].rearrange("p (m b t) -> p m b t", m=2, b=B)
                for b in range(B):
                    for m in range(2):
                        o = kb1[:, b, m, :] if w == 0 else z1[:, b, m, ZL:ZL + HALF]
                        last = v.tensor_tensor(o.rearrange("p (h t) -> p h t", h=8), spread(src[:, m, b, :], 1, [P, 8, NK]),
                                               spread(con[:, C_BD:C_BD + 8], 2, [P, 8, NK]), ALU.mult)
                last.then_inc(q["su1_dve"], 1)
            seq.sync()
            dve.wait_ge(q["gate_done"], 1)
            dve.wait_ge(q["ld_bo"], 16 * B)
            v.tensor_scalar(vo[BO_ROW:BO_ROW + 1, :, KC - 1, :], vo[BO_ROW:BO_ROW + 1, :, KC - 1, :],
                            gate[BO_ROW:BO_ROW + 1, 0:1], None, ALU.mult).then_inc(q["bo_done"], 1)

            def soft(i, k, pre):
                t = 2 * i + k
                after(dve, q[pre + "_tp"], 3 * t - 3)
                for u, (a, z) in enumerate(UNITS):
                    dve.wait_ge(q[pre + "_sc"], 3 * t + u + 1)
                    n = z - a
                    src = ps[:, u, 0:NK * n].rearrange("p (h t) -> p h t", h=n)
                    seq(v.tensor_reduce(mx[:, a:z], src, AX.X, ALU.max))
                    v.tensor_tensor(sc[k % 2][:, NK * a:NK * z].rearrange("p (h t) -> p h t", h=n), src,
                                    spread(mx[:, a:z], 2, [P, n, NK]), ALU.subtract).then_inc(q[pre + "_sub"], 1)

            def xn0(i, k, pre):
                t = 2 * i + k
                after(dve, q[pre + "_tx"], t - 1)
                norm(xn[k % 2], tile_of(i, k)).then_inc(q[pre + "_xn"], 1)

            def step0(i, k, prev=True, nxt=True):
                soft(i, k, "n")
                dve.wait_ge(q["n_exp"], 2 * i + k + 1)
                s3 = sc[k % 2].rearrange("p (h t) -> p h t", h=H)
                seq(v.tensor_reduce(den[:], s3, AX.X, ALU.add))
                seq(v.reciprocal(rden[:], den[:]))
                v.tensor_tensor(s3, s3, spread(rden[:], 2, [P, H, NK]), ALU.mult).then_inc(q["n_p"], 1)
                if prev:
                    res0(i, k - 1)
                if nxt:
                    xn0(i, k + 2, "n")
                if prev:
                    norm_stats(tile_of(i, k - 1))

            def res0(i, k):
                tile = tile_of(i, k)
                dve.wait_ge(q["n_pv"], 2 * i + k + 1)
                ins = v.tensor_tensor(xs[:, tile, :], xs[:, tile, :], ps[:, 6 + k % 2, 0:D], ALU.add)
                ins.then_inc(q["n_res"], 1)
                dve.wait_ge(q["n_res"], 2 * i + k + 1)

            dve.wait_ge(q["rstd_done"], 1)
            xn0(0, 0, "n")
            xn0(0, 1, "n")
            step0(0, 0, prev=False)
            step0(0, 1)
            with dve.Fori(1, TB - 1) as i:
                seq.enter(i - 1, 12)
                step0(i, 0)
                step0(i, 1)
            seq.leave(TB - 2)
            step0(TB - 1, 0, nxt=False)
            step0(TB - 1, 1, nxt=False)
            res0(TB - 1, 1)
            norm_stats(T - 1)

            variances(2)
            for t in range(T):
                g = t // 4
                after(dve, q["f_tx"], 2 * g - 2)
                norm(xng[g % 2][:, t % 4, :], t).then_inc(q["f_xn"], 1)
            dve.wait_ge(q["f_upd"], NG)
            cv = csum[:].rearrange("p m (b h) -> p m b h", h=2)
            seq(v.tensor_tensor(gcx[:], cv[:, :, :, 0], cv[:, :, :, 1], ALU.add))
            v.tensor_scalar(gcx[:], gcx[:], 1.0 / S, None, ALU.mult).then_inc(q["f_gcx"], 1)
            sgn = con[:, C_SG:C_SG + 1]
            seq(v.tensor_scalar(cpl[:, 3:4], par[:, V_AR:V_AR + 1], 0.7, None, ALU.mult))
            v.tensor_scalar(cpl[:, 0:1], par[:, V_AR:V_AR + 1], 0.3, sgn, ALU.mult, ALU.mult).then_inc(q["f_cpl"], 1)
            dve.wait_ge(q["f_a4"], 1)
            seq(v.tensor_scalar(cpl[:, 1:3], gtan[:], cpl[:, 3:4], 0.1, ALU.mult, ALU.add))
            seq(v.tensor_scalar(cpl[:, 1:3], cpl[:, 1:3], sgn, None, ALU.mult))
            with dve.Fori(0, 3) as c:
                seq.enter(c, 12)
                for g in range(NG):
                    n = 4 * c + g
                    dve.wait_ge(q["f_a4"], n + 2)
                    x0, x1 = st_x[:, 0, g, :], st_x[:, 1, g, :]
                    seq(v.tensor_scalar(cs, tt[g % 2], cpl[:, 0:1], cpl[:, 1 + g // 2:2 + g // 2], ALU.mult, ALU.add))
                    seq.mark(v.tensor_tensor(u0, cs, x1, ALU.mult))
                    seq(v.tensor_tensor(u1, cs, x0, ALU.mult))
                    v.tensor_tensor(x0, x0, u0, ALU.add)
                    v.tensor_tensor(x1, x1, u1, ALU.subtract).then_inc(q["f_upd"], 1)
                    dve.wait_ge(q["f_upd"], n + 5)
            seq.leave(3)
            for n in range(T // 2):
                dve.wait_ge(q["f_bt"], n + 1)
                xx = xs[:, 2 * n:2 * n + 2, :].rearrange("p t d -> p (t d)")
                v.scalar_tensor_tensor(xx, ps[:, n, :], gate[:, 2:3], xx, ALU.mult, ALU.add).then_inc(q["f_res"], 1)
                dve.wait_ge(q["f_res"], n + 1)
                norm_stats(2 * n)
                norm_stats(2 * n + 1)

            def att1(i, k):
                t = 2 * i + k
                dve.wait_ge(q["a_pv"], t + 1)
                o = ps[:, 6, 0:H * (HD + 1)].rearrange("p (h e) -> p h e", e=HD + 1)
                seq(v.reciprocal(rden[:], o[:, :, HD]))
                after(dve, q["a_at"], t)
                v.tensor_tensor(att.rearrange("p (h e) -> p h e", e=HD), o[:, :, 0:HD],
                                spread(rden[:], 2, [P, H, HD]), ALU.mult).then_inc(q["a_att"], 1)

            def res1(i, k):
                tile = tile_of(i, k)
                dve.wait_ge(q["a_wo"], 2 * i + k + 1)
                v.scalar_tensor_tensor(xs[:, tile, :], ps[:, 7, 0:D], gate[:, 1:2], xs[:, tile, :],
                                       ALU.mult, ALU.add).then_inc(q["a_res"], 1)
                dve.wait_ge(q["a_res"], 2 * i + k + 1)

            def step1(i, k, p1=True, p2=True, nxt=True):
                soft(i, k, "a")
                if p2:
                    res1(i, k - 2)
                if p1:
                    att1(i, k - 1)
                if p2:
                    norm_stats(tile_of(i, k - 2))
                if nxt:
                    xn0(i, k + 2, "a")

            variances(3)
            xn0(0, 0, "a")
            xn0(0, 1, "a")
            step1(0, 0, p1=False, p2=False)
            step1(0, 1, p2=False)
            step1(1, 0)
            step1(1, 1)
            with dve.Fori(2, TB - 1) as i:
                seq.enter(i - 2, 10)
                step1(i, 0)
                step1(i, 1)
            seq.leave(TB - 3)
            step1(TB - 1, 0, nxt=False)
            step1(TB - 1, 1, nxt=False)
            res1(TB - 1, 0)
            att1(TB - 1, 1)
            res1(TB - 1, 1)
            norm_stats(TB - 1)
            norm_stats(T - 1)

            variances(4)
            for t in range(T):
                norm(xn4[:, t, :], t).then_inc(q["r_xn"], 1)
            for g in range(NG):
                dve.wait_ge(q["r_lg"], g + 1)
                v.tensor_copy(lg[:, 4 * g:4 * g + 4, :],
                              ps[:, 4 + g, 0:4 * NE].rearrange("p (t e) -> p t e", e=NE)).then_inc(q["r_lgc"], 1)
            dve.wait_ge(q["r_lgc"], NG)
            full = [P, T, NE]
            rev = spread(con[:, C_RE:C_RE + NE], 1, full)

            def one_hot(o, scores, top):
                seq(v.tensor_reduce(top[:], scores[:], AX.X, ALU.max))
                seq(v.tensor_tensor(ra[:], scores[:], spread(top[:], 2, full), ALU.is_equal))
                seq(v.tensor_tensor(ra[:], ra[:], rev, ALU.mult))
                seq(v.tensor_reduce(r1[:], ra[:], AX.X, ALU.max))
                seq(v.tensor_tensor(o[:], ra[:], spread(r1[:], 2, full), ALU.is_equal))

            one_hot(oh[0], lg, m1)
            seq(v.scalar_tensor_tensor(lg2[:].rearrange("p t e -> p (t e)"), oh[0][:].rearrange("p t e -> p (t e)"),
                                       -BIG, lg[:].rearrange("p t e -> p (t e)"), ALU.mult, ALU.add))
            one_hot(oh[1], lg2, m2)
            v.tensor_tensor(msk[:], oh[0][:], oh[1][:], ALU.add).then_inc(q["r_mask"], 1)
            v.tensor_tensor(esc[:], lg[:], spread(m1[:], 2, full), ALU.subtract).then_inc(q["r_lgc"], 1)
            dve.wait_ge(q["r_e"], 2)
            seq(v.tensor_copy(tot[0][:], ps[:, 7, 0:T * NE].rearrange("p (t e) -> p t e", e=NE)))
            cur, step = 0, 1
            while step < T:
                seq.mark(v.tensor_copy(tot[1 - cur][:, 0:step, :], tot[cur][:, 0:step, :]))
                seq(v.tensor_tensor(tot[1 - cur][:, step:, :], tot[cur][:, step:, :], tot[cur][:, 0:T - step, :], ALU.add))
                cur, step = 1 - cur, 2 * step
            seq(v.tensor_tensor(cmp_[:], spread(tot[cur][:, T - 1, :], 2, [P, NE, T]),
                                spread(con[:, C_TH:C_TH + T], 1, [P, NE, T]), ALU.is_gt))
            seq(v.tensor_reduce(ntl[:], cmp_[:], AX.X, ALU.add))
            seq(v.tensor_copy(bs[0][:], ntl[:]))
            b0, step = 0, 1
            while step < NE:
                seq.mark(v.tensor_copy(bs[1 - b0][:, 0:step], bs[b0][:, 0:step]))
                seq(v.tensor_tensor(bs[1 - b0][:, step:], bs[b0][:, step:], bs[b0][:, 0:NE - step], ALU.add))
                b0, step = 1 - b0, 2 * step
            seq(v.tensor_tensor(scmp[:], spread(bs[b0][:], 1, [P, SLOTS, NE]),
                                spread(con[:, C_SL:C_SL + SLOTS], 2, [P, SLOTS, NE]), ALU.is_le))
            seq(v.tensor_reduce(sexp[:], scmp[:], AX.X, ALU.add))
            v.tensor_scalar(sei[:], sexp[:], float(NE - 1), None, ALU.min).then_inc(q["r_pos"], 1)
            seq(v.tensor_tensor(cnt[:], bs[b0][:], ntl[:], ALU.subtract))
            seq(v.tensor_scalar(cnt[:], cnt[:], float(P), None, ALU.mult))
            seq(v.tensor_tensor(rank[:], ps[:, 6, 0:T * NE].rearrange("p (t e) -> p t e", e=NE),
                                spread(cnt[:], 1, full), ALU.add))
            seq(v.tensor_tensor(rank[:, 1:, :], rank[:, 1:, :], tot[cur][:, 0:T - 1, :], ALU.add))
            for k in range(2):
                seq(v.tensor_tensor(ra[:], rank[:], oh[k][:], ALU.mult))
                seq(v.tensor_reduce(pos[:], ra[:], AX.X, ALU.add))
                seq.mark(v.tensor_copy(idx[k][:], pos[:]))
            seq.sync()
            v.tensor_copy(m1[:], m1[:]).then_inc(q["r_pos"], 1)
            seq(v.tensor_scalar(gw[:, 0:1], gate[:, 3:4], 1.0 / 3.0, None, ALU.mult))
            seq(v.tensor_scalar(gw[:, 1:2], gate[:, 3:4], 2.0 / 3.0, None, ALU.mult))
            seq(v.tensor_reduce(esum[:], esc[:], AX.X, ALU.add))
            seq(v.reciprocal(ersum[:], esum[:]))
            for k in range(2):
                seq(v.tensor_tensor(ra[:], esc[:], oh[k][:], ALU.mult))
                seq(v.tensor_reduce(wt[k][:], ra[:], AX.X, ALU.add))
                seq(v.tensor_tensor(wt[k][:], wt[k][:], ersum[:], ALU.mult))
                first = q["s_res" if k else "s_hs"]
                v.tensor_scalar(wt[k][:], wt[k][:], gw[:, 1:2], None, ALU.mult).then_inc(first, 1)
                dve.wait_ge(first, 1)

            def combine(i, k):
                t = 4 * i + k
                dve.wait_ge(q[f"c_ga{k % 4}"], 32 * (i + k // 4 + 1))
                w = [wt[r][:, bass.ds(t, 1)] for r in range(2)]
                xt_ = xs[:, bass.ds(t, 1), :].rearrange("p a d -> p (a d)")
                seq(v.scalar_tensor_tensor(xt_, ga[k % 4][0], w[0], xt_, ALU.mult, ALU.add))
                v.scalar_tensor_tensor(xt_, ga[k % 4][1], w[1], xt_, ALU.mult, ALU.add).then_inc(q["c_use"], 1)

            def shared(g0, g1, combining):
                with dve.Fori(g0, g1) as g:
                    if combining:
                        seq.enter(g - g0, 8)
                        dve.wait_ge(q["s_res"], 2 * g + 1)
                    for f in range(FC):
                        n = 4 * g + f
                        dve.wait_ge(q["s_h"], 2 * n + 2)
                        dve.wait_ge(q["s_sil"], n + 1)
                        dve.wait_ge(q["s_y"], 2 * g + 1)
                        v.tensor_tensor(hs[:, f, :], sil_s, ps[:, 2 * (f % 2) + 1, :], ALU.mult).then_inc(q["s_hs"], 1)
                        if combining:
                            for d in range(2):
                                combine(2 * (g - g0), 2 * f + d)
                    for u in range(2):
                        dve.wait_ge(q["s_y"], 2 * g + u + 2)
                        if combining:
                            dve.wait_ge(q["c_use"], 8 * (g - g0) + 8)
                        xx = xs[:, bass.ds(4 * g + 2 * u, 2), :].rearrange("p t d -> p (t d)")
                        v.scalar_tensor_tensor(xx, ps[:, 4 + u, :], gw[:, 0:1], xx, ALU.mult,
                                               ALU.add).then_inc(q["s_res"], 1)
                if combining:
                    seq.leave(g1 - g0)

            def e_ht(i, k):
                s = 2 * i + k
                dve.wait_ge(q["e_th"], 2 * s + 2)
                after(dve, q["e_y"], s - 1)
                v.tensor_copy(hT[k % 2][:, 2:4, :].rearrange("p f t -> p (f t)"),
                              ps[:, 6, 0:2 * P]).then_inc(q["e_hTv"], 1)

            def e_hh(i, k):
                s = 2 * i + k
                dve.wait_ge(q["e_h"], 2 * s + 2)
                dve.wait_ge(q["e_sil"], s + 1)
                after(dve, q["e_th"], 2 * s - 2)
                v.tensor_tensor(hh[k % 2], sil[k % 2], ps[:, 2 * (k % 2) + 1, :], ALU.mult).then_inc(q["e_hh"], 1)

            def e_y(i, k):
                s = 2 * i + k
                dve.wait_ge(q["e_y"], s + 1)
                after(dve, q[f"e_st{k % 2}"], 16 * (i + k // 2))
                v.tensor_copy(yo[k % 2], ps[:, 7, 0:D]).then_inc(q["e_yc"], 1)

            def e_step(i, k, prev=True):
                if prev:
                    e_ht(i, k - 1)
                e_hh(i, k)
                if prev:
                    e_y(i, k - 1)

            shared(0, NG // 2, False)
            e_step(0, 0, prev=False)
            e_step(0, 1)
            e_step(1, 0)
            e_step(1, 1)
            with dve.Fori(2, SLOTS // 2) as i:
                e_step(i, 0)
                e_step(i, 1)
            e_step(SLOTS // 2, 0)
            e_ht(SLOTS // 2, 0)
            e_y(SLOTS // 2, 0)
            shared(NG // 2, NG, True)


def kernel(**inputs):
    import numpy as np
    import concourse.bacc as bacc
    from concourse.bass_utils import run_bass_kernel_spmd as run

    a = {k: np.asarray(v) for k, v in inputs.items()}

    con = np.zeros((P, C_N), np.float32)
    row = np.arange(P)
    con[:, C_ID:C_ID + P] = np.eye(P)
    con[:, C_UP:C_UP + P] = row[:, None] < row[None, :]
    con[:, C_BD:C_BD + 8] = row[:, None] // HD == np.arange(8)[None, :]
    for c in range(KC):
        h0, n = heads_of(c)
        for j in range(n):
            con[:, C_IN + 3 * c + j] = (c * P + row) // NK == h0 + j
    con[:, C_RE:C_RE + NE] = NE - np.arange(NE)
    con[:, C_TH:C_TH + T] = P * np.arange(T)
    con[:, C_SL:C_SL + SLOTS] = np.arange(SLOTS)
    con[:, C_SG] = np.where(row < 64, 1.0, -1.0)

    small = np.zeros((P, V_N), np.float32)
    small[:, V_GX:V_GX + 2] = a["g_xattn"]
    small[:, V_GF:V_GF + 2] = a["g_ffn"]
    small[:, V_AR] = a["L0_ffn_adaptive_range"]
    small[:, V_GB3] = a["L0_ffn_gc_b3"]
    small[:, V_CB4] = a["L0_ffn_cn_b4"]
    small[:, V_CB1:V_CB1 + 2] = a["L0_ffn_cn_b1"].reshape(2, P).T
    small[:, V_CB2] = a["L0_ffn_cn_b2"]
    small[:64, V_CB3] = a["L0_ffn_cn_b3"]
    small[:, V_GB1] = a["L0_ffn_gc_b1"]
    small[:64, V_GB2] = a["L0_ffn_gc_b2"]
    for col, name in ((V_BK, "L0_xattn_bk"), (V_BV, "L0_xattn_bv"), (V_BQ, "L0_xattn_bq")):
        small[:, col:col + PAIRS] = a[name].reshape(PAIRS, P).T

    def columns(w):
        return w.transpose(1, 0, 2).reshape(D, H * DK)

    arrays = {
        "x": a["x"].reshape(B * S, D),
        "ctxT": a["ctx_1024"].reshape(B * NK, KD, P).transpose(2, 1, 0),
        "maskT": a["mask_BxSxS2_bk1"].transpose(2, 0, 1),
        "mask1": a["mask_BxS2_bk1"].reshape(1, B, NK),
        "consts": con, "small": small,
        "wk0": columns(a["L0_xattn_wk"]), "wv0": columns(a["L0_xattn_wv"]),
        "wq0T": a["L0_xattn_wq"].transpose(0, 2, 1).reshape(H * DK, D),
        "wo0": a["L0_xattn_wo"], "bo0": a["L0_xattn_bo"].reshape(1, D),
        "cw1": a["L0_ffn_cn_w1"], "cw2": a["L0_ffn_cn_w2"], "cw3": a["L0_ffn_cn_w3"],
        "cw4": np.broadcast_to(a["L0_ffn_cn_w4"], (64, P)),
        "gw1": a["L0_ffn_gc_w1"], "gw2": a["L0_ffn_gc_w2"], "gw3": np.broadcast_to(a["L0_ffn_gc_w3"], (64, P)),
        "wq1": a["L1_xattn_Wq"].T, "wk1": a["L1_xattn_Wk"].T, "wv1": a["L1_xattn_Wv"].T, "wo1": a["L1_xattn_Wo"].T,
        "wr": a["L1_ffn_w_router"], "w1": a["L1_ffn_w1"], "w3": a["L1_ffn_w3"], "w2": a["L1_ffn_w2"],
        "ws1": a["L1_ffn_ws1"], "ws3": a["L1_ffn_ws3"], "ws2": a["L1_ffn_ws2"],
    }
    nc = bacc.Bacc("TRN2", target_bir_lowering=False, num_devices=1)
    given, aps = {}, {}
    for name, value in arrays.items():
        value = np.ascontiguousarray(value)
        given[f"in_{name}"] = value
        aps[name] = nc.dram_tensor(f"in_{name}", value.shape, mybir.dt.from_np(value.dtype), kind="ExternalInput").ap()
    out = nc.dram_tensor("out_rows", (B * S, D), F32, kind="ExternalOutput").ap()
    build(nc, out=out, **aps)
    r = run(nc, [given], core_ids=[0])
    return r.results[0]["out_rows"].reshape(B, S, D)
```

```python
from contextlib import ExitStack

import concourse.bass as bass
from concourse import mybir

P = 128
B, S, D = 2, 1024, 256
T = B * S // P
TB = T // B
KD = D // P
NK = 77
H = 16
DK = 64
HD = D // H
PAIRS = H // 2
PW = 2 * NK
HK = H * NK
HALF = HK // 2
KC = (HK + P - 1) // P
LASTK = HK - (KC - 1) * P
BO_ROW = 96
UNITS = [(0, 6), (6, 12), (12, 16)]
PTG = [(0, 4), (4, 8), (8, KC)]
ZS = PW + P
ZN = PAIRS * ZS + P
ZL = 104
Z1 = ZL + HALF + 48
G4 = 512
NG = B * S // G4
NE = 8
F = 512
FC = F // P
GROUPS = [0, 8, 4, 12]
SLOTS = 2 * B * S // P + NE - 1
RW = D + 2
EPS = 1e-5
BIG = 1e30

F32 = mybir.dt.float32
BF16 = mybir.dt.bfloat16
I32 = mybir.dt.int32
U32 = mybir.dt.uint32
ALU = mybir.AluOpType
ACT = mybir.ActivationFunctionType
AX = mybir.AxisListType

C_ID = 0
C_UP = C_ID + P
C_BD = C_UP + P
C_IN = C_BD + 8
C_RE = C_IN + KC * 3
C_TH = C_RE + NE
C_SL = C_TH + T
C_SG = C_SL + SLOTS
C_TK = C_SG + 1
C_SP = C_TK + T
C_N = C_SP + 1

V_GX, V_GF, V_AR, V_GB3, V_CB4 = 0, 2, 4, 5, 6
V_CB1, V_CB2, V_CB3, V_GB1, V_GB2 = 7, 9, 10, 11, 12
V_BK, V_BV, V_BQ = 13, 21, 29
V_N = 37


def heads_of(c):
    last = min(c * P + P, HK) - 1
    return c * P // NK, last // NK - c * P // NK + 1


class Chain:

    def __init__(self, eng, sem):
        self.eng, self.sem, self.base, self.n = eng, sem, 0, 0

    def __call__(self, ins):
        ins.then_inc(self.sem, 1)
        self.n += 1
        self.eng.wait_ge(self.sem, self.base + self.n)

    def mark(self, ins):
        ins.then_inc(self.sem, 1)
        self.n += 1

    def sync(self):
        self.eng.wait_ge(self.sem, self.base + self.n)

    def enter(self, turn, each):
        self.at = self.n + (self.base if isinstance(self.base, int) else 0)
        self.base, self.n, self.each = self.at + turn * each, 0, each

    def leave(self, turns):
        assert self.n == self.each, (self.n, self.each)
        self.base, self.n = self.at + turns * self.each, 0


def after(eng, sem, value):
    if not isinstance(value, int) or value > 0:
        eng.wait_ge(sem, value)


def halves_of(c):
    h0, n = heads_of(c)
    return sorted({h0 // 8, (h0 + n - 1) // 8})


def spread(ap, axis, shape):
    return ap.unsqueeze(axis).to_broadcast(shape)


def build(nc, x, ctxT, maskT, mask1, consts, small, wk0, wv0, wq0T, wo0, bo0, cw1, cw2, cw3, cw4,
          gw1, gw2, gw3, wq1, wk1, wv1, wo1, wr, w1, w3, w2, ws1, ws3, ws2, out):
    st = ExitStack()
    with st:
        def sb(name, cols, dt=F32, rows=P):
            return st.enter_context(nc.sbuf_tensor(name, [rows] + (cols if isinstance(cols, list) else [cols]), dt))

        def sem(name):
            return st.enter_context(nc.semaphore(name))

        ps = st.enter_context(nc.psum_tensor("ps", [P, 8, 512], F32))

        xs = sb("x_rows", [T, D])
        con = sb("consts_sb", C_N)
        par = sb("params_sb", V_N)
        ctx = sb("ctx_sb", [KD, B * NK])
        early = sb("early", 2 * NE * KD * F)
        middle = sb("middle", NE * FC * D + T * RW)
        work = sb("work", 7424)
        late = sb("late", 7168)
        mrow_u8 = sb("mask_row_u8", [B, NK], mybir.dt.uint8, 1)
        mrf = sb("mask_row_f", [B, NK], rows=1); mval = sb("mask_valid", [4], rows=1)
        masks = sb("masks", 4 * HK // 2 + B * S // 2 + B * S // 4)
        stats = sb("stats", [T, 6]); mv = sb("mean_var", [T, 2])
        vare = sb("var_eps", T); rstd = sb("rstd", T); mhalf = sb("minus_half", T)
        mx = sb("maxes", H); den = sb("den", H); rden = sb("rden", H)
        gate = sb("gates", 4); gw = sb("gate_work", 8)
        ones_bf = sb("ones_bf", P, BF16)
        up_bf = sb("upper_bf", P, BF16)
        csum = sb("feature_sums", [KD, NG])
        gcx = sb("gc_x", [KD, B]); gh1 = sb("gc_h1", B); gh2 = sb("gc_h2", B, rows=64); gtan = sb("gc_tanh", B)
        cpl = sb("coupling", 4); hb = sb("half_biases", 2)

        def cut(region, at, shape):
            n = 1
            for s in shape:
                n *= s
            v = region[:, at:at + n]
            if len(shape) == 1:
                return v
            names = "abcd"[:len(shape)]
            return v.rearrange(f"p ({' '.join(names)}) -> p {' '.join(names)}", **dict(zip(names[1:], shape[1:])))

        ident = con[:, C_ID:C_ID + P]
        wk_s = cut(early, 0, [KD, H * DK]); wv_s = cut(early, 2048, [KD, H * DK])
        wq_s = cut(early, 4096, [PAIRS, D]); wo_s = cut(early, 6144, [PAIRS, D])
        kbd = cut(early, 8192, [B, PAIRS, PW])
        zv = cut(early, 8192 + B * PAIRS * PW, [B, ZN])
        z1 = cut(early, 0, [B, 2, Z1])
        w13 = cut(early, 0, [NE, 2, KD, F])
        gk = cut(middle, 0, [B, KD, HK])
        vo = cut(middle, B * KD * HK, [B, KC, D])
        st_x = cut(early, 0, [KD, NG, G4])
        xng = cut(early, 4096, [NG, 4, D])
        h1 = [cut(early, 8192 + 1024 * p, [2, G4]) for p in range(2)]
        h2 = [cut(early, 10240 + 512 * p, [G4]) for p in range(2)]
        h3 = [cut(early, 11264 + 512 * p, [G4]) for p in range(2)]
        tt = [cut(early, 12288 + 512 * p, [G4]) for p in range(2)]
        cs = cut(early, 13312, [G4]); u0 = cut(early, 13824, [G4]); u1 = cut(early, 14336, [G4])
        w2s = cut(middle, 0, [NE, FC, D])
        trow = cut(middle, NE * FC * D, [T, RW])
        xn4 = trow[:, :, 0:D]
        xn = [cut(work, 256 * p, [D]) for p in range(2)]
        xnT = [cut(work, 512 + 256 * p, [KD, P]) for p in range(2)]
        qT = [cut(work, 1024 + 256 * p, [KD, P]) for p in range(2)]
        sc = [cut(work, 1536 + HK * p, [HK]) for p in range(2)]
        pt = [cut(work, 4000 + KC * P * p, [KC, P]) for p in range(2)]
        att = cut(work, 6560, [D]); attT = cut(work, 6816, [KD, P])
        h = HK // 2
        mrhs = [masks[0:80, h * b:h * b + h].bitcast(BF16) for b in range(B)]
        mrow = [masks[0:1, h * (2 + b):h * (3 + b)].bitcast(BF16) for b in range(B)]
        mlhs = masks[0:80, 4 * h:4 * h + B * S // 2].bitcast(BF16).rearrange("p (b s) -> p b s", b=B)
        mask_u8 = masks[0:NK, 4 * h + B * S // 2:4 * h + B * S // 2 + B * S // 4].bitcast(
            mybir.dt.uint8).rearrange("p (b s) -> p b s", b=B)
        crow = cut(work, 1536, [B, HK])
        cb = middle[0:1, 10112:10112 + 3 * HK // 2].bitcast(BF16).rearrange("p (n k) -> p n k", n=3)
        kb1 = cut(late, 0, [B, 2, HALF])
        va = cut(late, B * 2 * HALF, [B, KC, 3, HD + 1])
        lw = B * 2 * HALF + B * KC * 3 * (HD + 1)
        wq1s = cut(late, lw, [KD, D]); wo1s = cut(late, lw + 512, [KD, D])
        wk1s = cut(late, lw + 1024, [KD, D]); wv1s = cut(late, lw + 1536, [KD, D])
        nets = lw + 2048
        fw1 = cut(late, nets, [KD, 256]); fw2 = cut(late, nets + 512, [KD, P]); fw3 = cut(late, nets + 768, [64])
        fw4 = late[0:64, nets + 832:nets + 960]
        gwt1 = cut(late, nets + 960, [KD, P]); gwt2 = cut(late, nets + 1216, [64])
        gwt3 = late[0:64, nets + 1280:nets + 1408]
        sw13 = cut(late, 0, [2, KD, F]); sw2 = cut(late, 2048, [FC, D]); xTs = cut(late, 3072, [NG, KD, G4])
        xT = [xTs[:, (o + 2) % NG, :, :] for o in range(NG)]
        sil_s = cut(work, 0, [G4]); hs = cut(work, 512, [FC, G4])
        xg = [cut(work, 2560 + RW * p, [RW]) for p in range(2)]
        xgT = [cut(work, 3076 + 256 * p, [KD, P]) for p in range(2)]
        sil = [cut(work, 3588 + 512 * p, [F]) for p in range(2)]
        hh = [cut(work, 4612 + 512 * p, [F]) for p in range(2)]
        hT = [cut(work, 512 * p, [FC, P]) for p in range(2)]
        yo = [cut(work, 1024 + 256 * p, [D]) for p in range(2)]
        wrs = sb("w_router", [KD, NE])
        lg, lg2, ra, oh0, oh1, esc, tot0, tot1, rank = [cut(masks, T * NE * n, [T, NE]) for n in range(9)]
        cmp_ = cut(masks, T * NE * 9, [NE, T]); scmp = cut(masks, T * NE * 10, [SLOTS, NE])
        oh, tot = [oh0, oh1], [tot0, tot1]
        m1 = sb("top1", T); m2 = sb("top2", T); r1 = sb("route_r", T)
        esum = sb("route_sum", T); ersum = sb("route_rsum", T)
        wt = [sb(f"route_w{k}", T) for k in range(2)]
        msk = sb("route_mask", [T, NE], BF16)
        cnt = sb("route_count", NE); ntl = sb("route_tiles", NE)
        bs = [sb(f"route_base{k}", NE) for k in range(2)]
        sexp = sb("slot_expert_f", SLOTS)
        sei = sb("slot_expert", SLOTS, I32)
        pos = sb("row_f", T)
        idx = [sb(f"row_index{k}", T, U32) for k in range(2)]
        spare = work[:, 7424 - RW:7424]
        slot_meta = sb("slot_tokens", [SLOTS, 2])
        turn = sb("turn", 1)
        to = [sb(f"out_index{k}", 1, U32) for k in range(2)]
        rows_in = nc.dram_tensor("expert_rows", (SLOTS * P, RW), F32, kind="Internal").ap()

        names = """ld_x ld_par ld_con pool_fill ld_ctx ld_k0 ld_k1 ld_q ld_v ld_o ld_mask ld_bo ld_ffn ld_l1 ld_crow ld_w13 ld_w2 ld_sh ld_sh2
        dve_seq pool_seq var_done rstd_done memset_done gate_done
        su_mm su_kv su_crow su_crow_bf su_g_mm su_g su_v_mm su_v bo_done ones_done su1_mm su1_dve su1_tm su1_t mask_done mrow_done
        n_xn n_tx n_xt n_sc n_sub n_exp n_p n_tp n_pt n_pv n_res
        f_xn f_tx f_gcx f_gmm f_gact f_l1 f_l2 f_l3 f_l4 f_a1 f_a2 f_a3 f_a4 f_upd f_bt f_res
        a_xn a_tx a_xt a_qm a_q a_sc a_sub a_exp a_tp a_pt a_pv a_att a_at a_atT a_wo a_res
        r_xn r_tx r_ev r_lg r_lgc r_e r_esc r_mask r_rank r_pos r_zero r_row r_scat0 r_scat1
        s_h s_sil s_hs s_y s_res e_ld0 e_ld1 e_tx e_xt e_h e_sil e_hh e_th e_hTa e_hTv e_y e_yc e_meta e_to e_turn e_add st_out""".split()
        q = {n: sem(n) for n in names}

        def tile_of(i, k):
            return i + k // 2 + (k % 2) * TB

        def ffn_group(n):
            return n // 2 % 2 + 2 * (n % 2)

        block = st.enter_context(nc.Block())

        @block.sync
        def _(sp):
            sp.dma_start(ctx[:], ctxT).then_inc(q["ld_ctx"], 16)
            for a, z in ((0, 3 * P), (3 * P, H * DK)):
                sp.dma_start(wk_s[:, :, a:z], wk0[:, a:z].rearrange("(k p) n -> p k n", p=P)).then_inc(q[f"ld_k{a // 384}"], 16)
            sp.dma_start(wv_s, wv0.rearrange("(k p) n -> p k n", p=P)).then_inc(q["ld_v"], 16)
            sp.dma_start(wq_s, wq0T.rearrange("(j p) n -> p j n", p=P)).then_inc(q["ld_q"], 16)
            sp.dma_start(wo_s, wo0.rearrange("(j p) n -> p j n", p=P)).then_inc(q["ld_o"], 16)
            for n in range(4):
                sp.dma_start(xs[:, 4 * n:4 * n + 4, :],
                             x[512 * n:512 * n + 512, :].rearrange("(t p) d -> p t d", p=P)).then_inc(q["ld_x"], 16)
            for dst, src in ((wk1s, wk1), (wv1s, wv1), (wq1s, wq1), (wo1s, wo1)):
                sp.dma_start(dst, src.rearrange("(k p) n -> p k n", p=P)).then_inc(q["ld_l1"], 16)
            for dst, src in ((fw1[:], cw1.rearrange("(k p) n -> p k n", p=P)),
                             (fw2[:], cw2.rearrange("(k p) n -> p k n", p=P)), (fw3[:], cw3), (fw4[:], cw4),
                             (gwt1[:], gw1.rearrange("(k p) n -> p k n", p=P)), (gwt2[:], gw2), (gwt3[:], gw3),
                             (wrs[:], wr.rearrange("(k p) n -> p k n", p=P))):
                sp.dma_start(dst, src).then_inc(q["ld_ffn"], 16)
            def bq_parts(b):
                sp.wait_ge(q["su_crow_bf"], b + 1)
                for n in range(3):
                    sp.dma_start(mrhs[b][NK + n:NK + n + 1, :], cb[:, n, :]).then_inc(q["ld_crow"], 16)
                sp.wait_ge(q["ld_crow"], 48 * (b + 1))

            bq_parts(0)
            sp.wait_ge(q["su_v"], B * KC // 2)
            for b in range(B):
                sp.dma_start(vo[BO_ROW:BO_ROW + 1, b, KC - 1, :], bo0).then_inc(q["ld_bo"], 16)
            bq_parts(1)
            sp.wait_ge(q["memset_done"], 1)
            for s in range(SLOTS):
                sp.dma_start(rows_in[s * P:(s + 1) * P, :], spare).then_inc(q["r_zero"], 16)
            sp.dma_start(out[T * P:(T + 1) * P, :], spare[:, 0:D]).then_inc(q["st_out"], 16)
            sp.wait_ge(q["n_pv"], T)
            for e in range(NE):
                sp.dma_start(w2s[:, e, :, :], w2[e].rearrange("(f p) d -> p f d", p=P)).then_inc(q["ld_w2"], 16)
            sp.wait_ge(q["f_bt"], T // 2)
            for e in range(NE):
                sp.dma_start(w13[:, e, 0, :, :], w1[e].rearrange("(k p) n -> p k n", p=P)).then_inc(q["ld_w13"], 16)
                sp.dma_start(w13[:, e, 1, :, :], w3[e].rearrange("(k p) n -> p k n", p=P)).then_inc(q["ld_w13"], 16)
            sp.wait_ge(q["a_sc"], 3 * T)
            sp.dma_start(sw13[:, 0, :, :], ws1.rearrange("(k p) n -> p k n", p=P)).then_inc(q["ld_sh"], 16)
            sp.dma_start(sw13[:, 1, :, :], ws3.rearrange("(k p) n -> p k n", p=P)).then_inc(q["ld_sh"], 16)
            sp.wait_ge(q["a_pv"], T)
            sp.dma_start(sw2, ws2.rearrange("(f p) d -> p f d", p=P)).then_inc(q["ld_sh2"], 16)

            def store(o):
                sp.wait_ge(q["s_res"], 2 * o + 2)
                t = GROUPS[o]
                sp.dma_start(out[t * P:(t + 4) * P, :].rearrange("(t p) d -> p t d", p=P),
                             xs[:, t:t + 4, :]).then_inc(q["st_out"], 16)

            for o in range(NG - 1):
                store(o)

            sp.wait_ge(q["r_scat0"], T * 16)
            sp.wait_ge(q["r_scat1"], T * 16)

            def load(i, k):
                s = 2 * i + k
                after(sp, q["e_tx"], s - 1)
                after(sp, q["e_meta"], s - 1)
                sp.dma_start(xg[k], rows_in[bass.ds(s * P, P), :]).then_inc(q[f"e_ld{k}"], 16)

            load(0, 0)
            load(0, 1)
            store(NG - 1)
            with sp.Fori(1, SLOTS // 2) as i:
                load(i, 0)
                load(i, 1)
            load(SLOTS // 2, 0)

        @block.gpsimd
        def _(pool):
            pool.dma_start(par[:], small).then_inc(q["ld_par"], 16)
            pool.dma_start(con[:], consts).then_inc(q["ld_con"], 16)
            pool.dma_start(mask_u8[:], maskT).then_inc(q["ld_mask"], 16)
            pool.dma_start(mrow_u8[:], mask1).then_inc(q["ld_mask"], 16)
            nc.gpsimd.memset(zv.rearrange("p b n -> p (b n)"), 0.0).then_inc(q["pool_fill"], 1)
            nc.gpsimd.memset(mlhs[:], 1.0).then_inc(q["pool_fill"], 1)
            nc.gpsimd.memset(mhalf[:], -0.5).then_inc(q["pool_seq"], 1)
            pool.wait_ge(q["pool_seq"], 1)
            for n in range(7):
                pool.wait_ge(q["var_done"], n + 1)
                nc.gpsimd.tensor_tensor(rstd[:], vare[:], mhalf[:], ALU.pow).then_inc(q["rstd_done"], 1)
            pool.wait_ge(q["r_zero"], 16 * SLOTS)
            for k in range(2):
                pool.wait_ge(q["r_row"], k + 1)
                for t in range(T):
                    pool.indirect_dma_start(rows_in[:, :], bass.IndirectOffsetOnAxis(ap=idx[k][:, t:t + 1], axis=0),
                                            trow[:, t, :], None).then_inc(q[f"r_scat{k}"], 16)

            def accumulate(i, k):
                s = 2 * i + k
                pool.wait_ge(q["e_yc"], s + 1)
                after(pool, q["e_add"], 16 * s)
                after(pool, q["e_turn"], s)
                nc.gpsimd.tensor_tensor(turn[:], mhalf[:, 0:1], mhalf[:, 0:1], ALU.mult).then_inc(q["e_turn"], 1)
                pool.indirect_dma_start(out[:, :], bass.IndirectOffsetOnAxis(ap=to[k][:, 0:1], axis=0),
                                        yo[k], None, compute_op=ALU.add).then_inc(q["e_add"], 16)

            pool.wait_ge(q["st_out"], 16 * (NG + 1))
            accumulate(0, 0)
            accumulate(0, 1)
            with pool.Fori(1, SLOTS // 2) as i:
                accumulate(i, 0)
                accumulate(i, 1)
            accumulate(SLOTS // 2, 0)
            pool.wait_ge(q["e_add"], 16 * SLOTS)

        @block.tensor
        def _(pe):
            def mm(o, l, r, start=True, stop=True, **kw):
                return nc.tensor.matmul(o, l, r, start=start, stop=stop, **kw)

            def tr(o, i, rows=P):
                return nc.tensor.transpose(o, i, ident[0:rows, 0:rows])

            pe.wait_ge(q["ld_ctx"], 16)
            pe.wait_ge(q["ld_k0"], 16)
            for w, ws in enumerate((wk_s, wv_s)):
                for u in range(3):
                    if u == 1 - w:
                        pe.wait_ge(q["ld_v" if w else "ld_k1"], 16)
                    for j in range(3 * u, min(3 * u + 3, PAIRS)):
                        o = ps[:, 3 * w + u, PW * (j - 3 * u):PW * (j - 3 * u) + PW]
                        for k in range(KD):
                            last = mm(o, ws[:, k, P * j:P * j + P], ctx[:, k, :], k == 0, k == KD - 1)
                    last.then_inc(q["su_mm"], 1)
            pe.wait_ge(q["ld_q"], 16)
            pe.wait_ge(q["ld_par"], 16)

            def bq_k(b):
                for u in range(3):
                    for j in range(3 * u, min(3 * u + 3, PAIRS)):
                        o = ps[0:1, u, PW * (j - 3 * u):PW * (j - 3 * u) + PW]
                        last = mm(o, par[:, V_BQ + j:V_BQ + j + 1], kbd[:, b, j, :])
                    last.then_inc(q["su_mm"], 1)

            pe.wait_ge(q["su_kv"], 3)
            bq_k(0)
            pe.wait_ge(q["su_kv"], 6)
            for n in range(6 * B):
                b, m, u = n // 6, n // 3 % 2, n % 3
                after(pe, q["su_g"], n - 4)
                for j in range(3 * u, min(3 * u + 3, PAIRS)):
                    o = ps[:, 3 + n % 5, PW * (j - 3 * u):PW * (j - 3 * u) + PW]
                    last = mm(o, wq_s[:, j, P * m:P * m + P], kbd[:, b, j, :])
                last.then_inc(q["su_g_mm"], 1)
            pe.wait_ge(q["su_crow"], 1)
            bq_k(1)
            pe.wait_ge(q["ld_l1"], 64)
            pe.wait_ge(q["su_g"], 6 * B)
            for w, ws in enumerate((wk1s, wv1s)):
                for m in range(2):
                    for k in range(KD):
                        last = mm(ps[:, 3 + w, PW * m:PW * m + PW], ws[:, k, P * m:P * m + P], ctx[:, k, :],
                                  k == 0, k == KD - 1)
                last.then_inc(q["su1_mm"], 1)
            pe.wait_ge(q["ld_o"], 16)
            for b in range(B):
                for n in range(KC // 2):
                    m = b * (KC // 2) + n
                    after(pe, q["su_v"], m - 2)
                    for c in (2 * n, 2 * n + 1):
                        js = range(c * P // PW, (min(c * P + P, HK) - 1) // PW + 1)
                        for j in js:
                            at = P + ZS * j + c * P - PW * j
                            last = mm(ps[:, 5 + m % 3, D * (c % 2):D * (c % 2) + D], zv[:, b, at:at + P],
                                      wo_s[:, j, :], j == js[0], j == js[-1])
                    last.then_inc(q["su_v_mm"], 1)
            pe.wait_ge(q["su1_dve"], 2)
            pe.wait_ge(q["su_crow"], 2)
            pe.wait_ge(q["ld_con"], 16)
            for b in range(B):
                for c in range(KC):
                    n = KC * b + c
                    after(pe, q["su1_t"], n - 3)
                    for m in halves_of(c):
                        at = ZL + c * P - HALF * m
                        last = tr(ps[:, n % 4, P * m:P * m + P], z1[:, b, m, at:at + P])
                    last.then_inc(q["su1_tm"], 1)

            def xt(i, k, pre):
                t = 2 * i + k
                pe.wait_ge(q[pre + "_xn"], t + 1)
                after(pe, q["n_xt" if pre == "n" else "a_q"], t)
                for m in range(KD):
                    last = tr(ps[:, 5, P * m:P * m + P], xn[k % 2][:, P * m:P * m + P])
                last.then_inc(q[pre + "_tx"], 1)

            def trans_p(i, k, pre, ready, groups=(0, 1, 2)):
                t = 2 * i + k
                pe.wait_ge(q[pre + ready], t + 1)
                for j in groups:
                    c0, c1 = PTG[j]
                    after(pe, q[pre + "_pt"], 3 * t + j - 1)
                    for c in range(c0, c1):
                        w = min(P, HK - P * c)
                        last = tr(ps[0:w, 3 + (k + j) % 2, P * (c - c0):P * (c - c0) + P],
                                  sc[k % 2][:, P * c:P * c + w])
                    last.then_inc(q[pre + "_tp"], 1)

            def scores0(i, k):
                t = 2 * i + k
                p = k % 2
                pe.wait_ge(q["n_xt"], t + 1)
                for u, (a, z) in enumerate(UNITS):
                    after(pe, q["n_sub"], 3 * t - 2 + u)
                    n = NK * (z - a)
                    for m in range(KD):
                        mm(ps[:, u, 0:n], xnT[p][:, m, :], gk[:, p, m, NK * a:NK * z], m == 0, False)
                    mm(ps[:, u, 0:n], mlhs[:, p, bass.ds((i + k // 2) * P, P)], mrhs[p][:, NK * a:NK * z],
                       False, True).then_inc(q["n_sc"], 1)

            def pv0(i, k):
                t = 2 * i + k
                p = k % 2
                after(pe, q["n_res"], t - 1)
                for c in range(KC):
                    if c % 4 == 0:
                        pe.wait_ge(q["n_pt"], 3 * t + c // 4 + 1)
                    last = mm(ps[:, 6 + p, 0:D], pt[p][:, c, :], vo[:, p, c, :], c == 0, c == KC - 1)
                last.then_inc(q["n_pv"], 1)

            def step0(i, k, prev=True, nxt=True):
                scores0(i, k)
                if prev:
                    trans_p(i, k - 1, "n", "_p")
                if nxt:
                    xt(i, k + 1, "n")
                if prev:
                    pv0(i, k - 1)

            pe.wait_ge(q["su_v"], B * KC // 2)
            pe.wait_ge(q["ld_crow"], 48)
            pe.wait_ge(q["mask_done"], 1)
            pe.wait_ge(q["su1_t"], B * KC)
            xt(0, 0, "n")
            step0(0, 0, prev=False)
            pe.wait_ge(q["ld_crow"], 48 * B)
            pe.wait_ge(q["bo_done"], 1)
            step0(0, 1)
            step0(1, 0)
            step0(1, 1)
            with pe.Fori(2, TB - 1) as i:
                step0(i, 0)
                step0(i, 1)
            step0(TB - 1, 0)
            step0(TB - 1, 1, nxt=False)

            def to_columns(n, banks):
                g = ffn_group(n)
                pe.wait_ge(q["f_xn"], 4 * n + 4)
                for m in range(KD):
                    for j in range(4):
                        last = tr(ps[:, banks[m], P * j:P * j + P], xng[:, g, j, P * m:P * m + P])
                    last.then_inc(q["f_tx"], 1)

            def net1(n):
                g = ffn_group(n)
                pe.wait_ge(q["f_upd"], n + 1)
                for o in range(2):
                    for m in range(KD):
                        last = mm(ps[:, 4 * (n % 2) + o, :], fw1[:, m, P * o:P * o + P], st_x[:, m, g, :],
                                  m == 0, m == KD - 1)
                    last.then_inc(q["f_l1"], 1)

            def net2(n):
                pe.wait_ge(q["f_a1"], 2 * n + 2)
                after(pe, q["f_a4"], n - 1)
                for m in range(KD):
                    last = mm(ps[:, 4 * (n % 2) + 2, :], fw2[:, m, :], h1[n % 2][:, m, :], m == 0, m == KD - 1)
                last.then_inc(q["f_l2"], 1)

            def net3(n):
                pe.wait_ge(q["f_a2"], n + 1)
                mm(ps[0:64, 4 * (n % 2) + 3, :], fw3[:], h2[n % 2]).then_inc(q["f_l3"], 1)

            def net4(n):
                pe.wait_ge(q["f_a3"], n + 1)
                mm(ps[:, 4 * (n % 2) + 2, :], fw4[:], h3[n % 2][0:64, :]).then_inc(q["f_l4"], 1)

            def to_rows(n, banks):
                g = ffn_group(n)
                pe.wait_ge(q["f_upd"], 2 * NG + n + 5)
                for u in range(2):
                    for j in range(2):
                        for m in range(KD):
                            at = P * (2 * u + j)
                            last = tr(ps[:, banks[u], D * j + P * m:D * j + P * m + P], st_x[:, m, g, at:at + P])
                    last.then_inc(q["f_bt"], 1)

            pe.wait_ge(q["n_sub"], 3 * T)
            pe.wait_ge(q["n_xt"], T)
            to_columns(0, (0, 1))
            to_columns(1, (2, 5))
            trans_p(TB - 1, 1, "n", "_p")
            pe.wait_ge(q["ld_ffn"], 128)
            net1(0)
            pv0(TB - 1, 1)
            pe.wait_ge(q["n_pt"], 3 * T)
            net1(1)
            net2(0)
            pe.wait_ge(q["n_res"], T)
            net2(1)
            to_columns(2, (0, 1))
            to_columns(3, (4, 5))
            net3(0)
            net3(1)
            net4(0)
            net4(1)
            pe.wait_ge(q["f_gcx"], 1)
            for m in range(KD):
                last = mm(ps[:, 3, 0:B], gwt1[:, m, :], gcx[:, m, :], m == 0, m == KD - 1)
            last.then_inc(q["f_gmm"], 1)
            net1(2)
            pe.wait_ge(q["f_gact"], 1)
            mm(ps[0:64, 3, 0:B], gwt2[:], gh1[:]).then_inc(q["f_gmm"], 1)
            net1(3)
            pe.wait_ge(q["f_gact"], 2)
            mm(ps[:, 3, 0:B], gwt3[:], gh2[:]).then_inc(q["f_gmm"], 1)
            net2(2)
            net2(3)
            pe.wait_ge(q["f_gact"], 3)
            net3(2)
            net3(3)
            net4(2)
            net4(3)
            for n in range(4, 10, 2):
                for net in (net1, net2, net3, net4):
                    net(n)
                    net(n + 1)
            net1(10)
            net1(11)
            to_rows(0, (3, 7))
            net2(10)
            net2(11)
            to_rows(1, (0, 1))
            pe.wait_ge(q["f_res"], 2)
            net3(10)
            net3(11)
            net4(10)
            net4(11)

            def queries(i, k):
                t = 2 * i + k
                pe.wait_ge(q["a_xt"], t + 1)
                for o in range(2):
                    for m in range(KD):
                        last = mm(ps[:, 5, P * o:P * o + P], wq1s[:, m, P * o:P * o + P], xnT[k % 2][:, m, :],
                                  m == 0, m == KD - 1)
                last.then_inc(q["a_qm"], 1)

            def scores1(i, k):
                t = 2 * i + k
                p = k % 2
                pe.wait_ge(q["a_q"], t + 1)
                for u, (a, z) in enumerate(UNITS):
                    after(pe, q["a_sub"], 3 * t - 2 + u)
                    c0, c1 = NK * a, NK * z
                    mm(ps[:, u, 0:c1 - c0], ones_bf[0:1, :], mrow[p][:, c0:c1], True, True)
                    parts = [(m, max(c0, HALF * m), min(c1, HALF * (m + 1))) for m in range(2)]
                    parts = [x for x in parts if x[1] < x[2]]
                    for m, x0, x1 in parts:
                        last = mm(ps[:, u, x0 - c0:x1 - c0], qT[p][:, m, :], kb1[:, p, m, x0 - HALF * m:x1 - HALF * m],
                                  False, True, skip_group_check=True)
                    last.then_inc(q["a_sc"], 1)

            def pv1(i, k):
                t = 2 * i + k
                p = k % 2
                after(pe, q["a_att"], t)
                for c in range(KC):
                    if c % 4 == 0:
                        pe.wait_ge(q["a_pt"], 3 * t + c // 4 + 1)
                    h0, n = heads_of(c)
                    last = mm(ps[:, 6, 17 * h0:17 * (h0 + n)], pt[p][:, c, :], va[:, p, c, 0:n, :],
                              c == 0, True, skip_group_check=True)
                last.then_inc(q["a_pv"], 1)

            def att_t(i, k):
                t = 2 * i + k
                pe.wait_ge(q["a_att"], t + 1)
                after(pe, q["a_res"], t)
                for m in range(KD):
                    last = tr(ps[:, 7, P * m:P * m + P], att[:, P * m:P * m + P])
                last.then_inc(q["a_at"], 1)

            def out1(i, k):
                t = 2 * i + k
                pe.wait_ge(q["a_atT"], t + 1)
                for m in range(KD):
                    last = mm(ps[:, 7, 0:D], attT[:, m, :], wo1s[:, m, :], m == 0, m == KD - 1)
                last.then_inc(q["a_wo"], 1)

            def step1(i, k, p1=True, p2=True, nxt=True):
                scores1(i, k)
                if p1:
                    trans_p(i, k - 1, "a", "_exp", (0, 1))
                if p2:
                    att_t(i, k - 2)
                if nxt:
                    xt(i, k + 1, "a")
                if p1:
                    trans_p(i, k - 1, "a", "_exp", (2,))
                    pv1(i, k - 1)
                if nxt:
                    queries(i, k + 1)
                if p2:
                    out1(i, k - 2)

            xt(0, 0, "a")
            queries(0, 0)
            pe.wait_ge(q["mrow_done"], 1)
            pe.wait_ge(q["f_res"], 4)
            pe.wait_ge(q["f_a4"], 11)
            step1(0, 0, p1=False, p2=False)
            to_rows(2, (3, 4))
            pe.wait_ge(q["f_a4"], 12)
            to_rows(3, (6, 7))
            pe.wait_ge(q["f_res"], 8)
            step1(0, 1, p2=False)
            step1(1, 0)
            step1(1, 1)
            with pe.Fori(2, TB - 1) as i:
                step1(i, 0)
                step1(i, 1)
            step1(TB - 1, 0)
            step1(TB - 1, 1, nxt=False)

            def router_xt(o, bank):
                pe.wait_ge(q["r_xn"], 4 * o + 4)
                for m in range(KD):
                    for j in range(4):
                        last = tr(ps[:, bank + m, P * j:P * j + P], xn4[:, GROUPS[o] + j, P * m:P * m + P])
                    last.then_inc(q["r_tx"], 1)

            def logits(o, bank):
                pe.wait_ge(q["r_ev"], 2 * o + 2)
                for j in range(4):
                    at = NE * (4 * (o % 2) + j)
                    for m in range(KD):
                        last = mm(ps[:, bank, at:at + NE], xT[o][:, m, P * j:P * j + P], wrs[:, m, :],
                                  m == 0, m == KD - 1)
                last.then_inc(q["r_lg"], 1)

            trans_p(TB - 1, 1, "a", "_exp")
            att_t(TB - 1, 0)
            pv1(TB - 1, 1)
            out1(TB - 1, 0)
            pe.wait_ge(q["a_sub"], 3 * T)
            router_xt(0, 0)
            pe.wait_ge(q["a_pt"], 3 * T)
            att_t(TB - 1, 1)
            router_xt(1, 2)
            out1(TB - 1, 1)
            logits(0, 5)
            logits(1, 5)

            def s_up(o, f):
                n = 4 * o + f
                after(pe, q["s_hs"], n - 1)
                for w in range(2):
                    for m in range(KD):
                        last = mm(ps[:, 2 * (f % 2) + w, :], sw13[:, w, m, P * f:P * f + P],
                                  xT[o][:, m, :], m == 0, m == KD - 1)
                    last.then_inc(q["s_h"], 1)

            def s_down(o, u):
                pe.wait_ge(q["s_hs"], 4 * o + 4)
                after(pe, q["s_res"], 2 * o + u - 1)
                for j in range(2):
                    for f in range(FC):
                        at = P * (2 * u + j)
                        last = mm(ps[:, 4 + u, D * j:D * j + D], hs[:, f, at:at + P], sw2[:, f, :],
                                  f == 0, f == FC - 1)
                last.then_inc(q["s_y"], 1)

            pe.wait_ge(q["ld_sh"], 32)
            s_up(0, 0)
            s_up(0, 1)
            pe.wait_ge(q["a_res"], T)
            router_xt(2, 6)
            pe.wait_ge(q["r_lgc"], 1)
            router_xt(3, 4)
            s_up(0, 2)
            logits(2, 6)
            logits(3, 6)
            s_up(0, 3)
            pe.wait_ge(q["ld_sh2"], 16)
            s_down(0, 0)
            pe.wait_ge(q["r_lgc"], 2)
            pe.wait_ge(q["r_mask"], 1)
            rhs = msk[:].rearrange("p t e -> p (t e)")
            mm(ps[:, 6, 0:T * NE], up_bf[:], rhs).then_inc(q["r_rank"], 1)
            mm(ps[:, 7, 0:T * NE], ones_bf[:], rhs).then_inc(q["r_rank"], 1)
            s_down(0, 1)
            for o in range(1, NG):
                for f in range(FC):
                    s_up(o, f)
                for u in range(2):
                    s_down(o, u)

            def e_trans(i, k):
                s = 2 * i + k
                pe.wait_ge(q[f"e_ld{k % 2}"], 16 * (i + k // 2 + 1))
                after(pe, q["e_xt"], s)
                for m in range(KD):
                    last = tr(ps[:, 4, P * m:P * m + P], xg[k % 2][:, P * m:P * m + P])
                last.then_inc(q["e_tx"], 1)

            def expert_of(s):
                return pe.value_load(sei[0:1, bass.ds(s, 1)], min_val=0, max_val=NE - 1)

            def e_up(i, k, lagging=None):
                s = 2 * i + k
                p = k % 2
                pe.wait_ge(q["e_xt"], s + 1)
                after(pe, q["e_hh"], s - 1)
                e = expert_of(s)
                for w in range(2):
                    for m in range(KD):
                        last = mm(ps[:, 2 * p + w, :], xgT[p][:, m, :],
                                  w13[:, bass.ds(e, 1), w, m, :].rearrange("p a n -> p (a n)"), m == 0, m == KD - 1)
                    last.then_inc(q["e_h"], 1)
                    if w == 0 and lagging is not None:
                        lagging = expert_of(lagging)
                return lagging

            def e_hidden_t(i, k):
                s = 2 * i + k
                pe.wait_ge(q["e_hh"], s + 1)
                after(pe, q["e_hTa"], s)
                after(pe, q["e_hTv"], s)
                for u in range(2):
                    for f in range(2):
                        last = tr(ps[:, 5 + u, P * f:P * f + P], hh[k % 2][:, P * (2 * u + f):P * (2 * u + f) + P])
                    last.then_inc(q["e_th"], 1)

            def e_down(i, k, e=None):
                s = 2 * i + k
                if e is None:
                    e = expert_of(s)
                pe.wait_ge(q["e_hTa"], s + 1)
                pe.wait_ge(q["e_hTv"], s + 1)
                after(pe, q["e_yc"], s)
                for f in range(FC):
                    last = mm(ps[:, 7, 0:D], hT[k % 2][:, f, :],
                              w2s[:, bass.ds(e, 1), f, :].rearrange("p a n -> p (a n)"), f == 0, f == FC - 1)
                last.then_inc(q["e_y"], 1)

            def e_step(i, k, p1=True, p2=True, nxt=True):
                e = e_up(i, k, 2 * i + k - 2 if p2 else None)
                if p1:
                    e_hidden_t(i, k - 1)
                if nxt:
                    e_trans(i, k + 1)
                if p2:
                    e_down(i, k - 2, e)

            pe.wait_ge(q["ld_w13"], 32 * NE)
            pe.wait_ge(q["ld_w2"], 16 * NE)
            pe.wait_ge(q["s_hs"], 4 * NG)
            pe.wait_ge(q["s_res"], 2 * NG - 1)
            e_trans(0, 0)
            e_step(0, 0, p1=False, p2=False)
            e_step(0, 1, p2=False)
            e_step(1, 0)
            e_step(1, 1)
            with pe.Fori(2, SLOTS // 2) as i:
                e_step(i, 0)
                e_step(i, 1)
            e_step(SLOTS // 2, 0, nxt=False)
            e_hidden_t(SLOTS // 2, 0)
            e_down(SLOTS // 2, -1)
            e_down(SLOTS // 2, 0)

        @block.scalar
        def _(act):
            def copy(o, i):
                return nc.scalar.activation(o, i, ACT.Copy)

            act.wait_ge(q["ld_par"], 16)
            nc.scalar.activation(gate[:], par[:, V_GX:V_GX + 4], ACT.Tanh).then_inc(q["gate_done"], 1)
            def bq_row(b):
                act.wait_ge(q["su_mm"], 6 + 3 * (b + 1))
                for u, (a, z) in enumerate(UNITS):
                    last = copy(crow[0:1, b, NK * a:NK * z], ps[0:1, u, 0:NK * (z - a)])
                last.then_inc(q["su_crow"], 1)

            bq_row(0)
            for n in range(12):
                b, m, u = n // 6, n // 3 % 2, n % 3
                a, z = UNITS[u]
                act.wait_ge(q["su_g_mm"], n + 1)
                copy(gk[:, b, m, NK * a:NK * z], ps[:, 3 + n % 5, 0:NK * (z - a)]).then_inc(q["su_g"], 1)
            bq_row(1)
            act.wait_ge(q["gate_done"], 1)
            for n in range(B * KC // 2):
                b, c = n // (KC // 2), 2 * (n % (KC // 2))
                act.wait_ge(q["su_v_mm"], n + 1)
                nc.scalar.activation(vo[:, b, c:c + 2, :].rearrange("p c d -> p (c d)"), ps[:, 5 + n % 3, :],
                                     ACT.Copy, scale=gate[:, 0:1]).then_inc(q["su_v"], 1)
            act.wait_ge(q["ones_done"], B)
            for n in range(B * KC):
                b, c = n // KC, n % KC
                h0, nh = heads_of(c)
                act.wait_ge(q["su1_tm"], n + 1)
                for m in halves_of(c):
                    a, z = max(h0, 8 * m), min(h0 + nh, 8 * m + 8)
                    src = ps[:, n % 4, P * m + HD * (a - 8 * m):P * m + HD * (z - 8 * m)]
                    last = copy(va[:, b, c, a - h0:z - h0, 0:HD], src.rearrange("p (h d) -> p h d", d=HD))
                last.then_inc(q["su1_t"], 1)

            def ev_xt(i, k, pre, used):
                t = 2 * i + k
                act.wait_ge(q[pre + "_tx"], t + 1)
                if used == "n_sc":
                    after(act, q["n_sc"], 3 * t - 3)
                else:
                    after(act, q["a_qm"], t - 1)
                copy(xnT[k % 2].rearrange("p k t -> p (k t)"), ps[:, 5, 0:D]).then_inc(q[pre + "_xt"], 1)

            def ev_pt(i, k, pre, groups=(0, 1, 2)):
                t = 2 * i + k
                after(act, q[pre + "_pv"], t - 1)
                for j in groups:
                    c0, c1 = PTG[j]
                    act.wait_ge(q[pre + "_tp"], 3 * t + j + 1)
                    bank = ps[:, 3 + (k + j) % 2, :]
                    if c1 < KC:
                        last = copy(pt[k % 2][:, c0:c1, :].rearrange("p c t -> p (c t)"), bank[:, 0:P * (c1 - c0)])
                    else:
                        copy(pt[k % 2][:, c0, :], bank[:, 0:P])
                        last = copy(pt[k % 2][0:LASTK, c0 + 1, :], bank[0:LASTK, P:2 * P])
                    last.then_inc(q[pre + "_pt"], 1)

            def exps(i, k, pre, scale):
                t = 2 * i + k
                act.wait_ge(q[pre + "_sub"], 3 * t + 3)
                nc.scalar.activation(sc[k % 2], sc[k % 2], ACT.Exp, scale=scale).then_inc(q[pre + "_exp"], 1)

            def step0(i, k, prev=True, nxt=True):
                if prev:
                    ev_pt(i, k - 1, "n")
                if nxt:
                    ev_xt(i, k + 1, "n", "n_sc")
                exps(i, k, "n", DK ** -0.5)

            ev_xt(0, 0, "n", "n_sc")
            step0(0, 0, prev=False)
            step0(0, 1)
            step0(1, 0)
            step0(1, 1)
            with act.Fori(2, TB - 1) as i:
                step0(i, 0)
                step0(i, 1)
            step0(TB - 1, 0)
            step0(TB - 1, 1, nxt=False)

            def state(n, banks):
                g = ffn_group(n)
                for m in range(KD):
                    act.wait_ge(q["f_tx"], 2 * n + m + 1)
                    last = nc.scalar.activation(st_x[:, m, g, :], ps[:, banks[m], :], ACT.Copy,
                                                accum_out=csum[:, m, g:g + 1])
                last.then_inc(q["f_upd"], 1)

            def act1(n):
                for o in range(2):
                    act.wait_ge(q["f_l1"], 2 * n + o + 1)
                    nc.scalar.activation(h1[n % 2][:, o, :], ps[:, 4 * (n % 2) + o, :], ACT.Gelu,
                                         bias=par[:, V_CB1 + o:V_CB1 + o + 1]).then_inc(q["f_a1"], 1)

            def act2(n):
                act.wait_ge(q["f_l2"], n + 1)
                nc.scalar.activation(h2[n % 2], ps[:, 4 * (n % 2) + 2, :], ACT.Gelu,
                                     bias=par[:, V_CB2:V_CB2 + 1]).then_inc(q["f_a2"], 1)

            def act3(n):
                act.wait_ge(q["f_l3"], n + 1)
                nc.scalar.activation(h3[n % 2][0:64, :], ps[0:64, 4 * (n % 2) + 3, :], ACT.Gelu,
                                     bias=par[0:64, V_CB3:V_CB3 + 1]).then_inc(q["f_a3"], 1)

            def act4(n):
                act.wait_ge(q["f_l4"], n + 1)
                if n >= 2:
                    act.wait_ge(q["f_upd"], n + 3)
                nc.scalar.activation(tt[n % 2], ps[:, 4 * (n % 2) + 2, :], ACT.Tanh, bias=hb[:, 1:2],
                                     scale=0.5).then_inc(q["f_a4"], 1)

            state(0, (0, 1))
            state(1, (2, 5))
            ev_pt(TB - 1, 1, "n")
            act1(0)
            act1(1)
            act2(0)
            act2(1)
            state(2, (0, 1))
            state(3, (4, 5))
            act3(0)
            act3(1)
            act4(0)
            act4(1)
            act.wait_ge(q["f_gmm"], 1)
            nc.scalar.activation(gh1[:], ps[:, 3, 0:B], ACT.Gelu, bias=par[:, V_GB1:V_GB1 + 1]).then_inc(q["f_gact"], 1)
            act1(2)
            act.wait_ge(q["f_gmm"], 2)
            nc.scalar.activation(gh2[:], ps[0:64, 3, 0:B], ACT.Gelu,
                                 bias=par[0:64, V_GB2:V_GB2 + 1]).then_inc(q["f_gact"], 1)
            act1(3)
            act.wait_ge(q["f_gmm"], 3)
            nc.scalar.activation(gtan[:], ps[:, 3, 0:B], ACT.Tanh, bias=hb[:, 0:1], scale=0.5).then_inc(q["f_gact"], 1)
            for a in (act2, act3, act4):
                a(2)
                a(3)
            for n in range(4, 12, 2):
                for a in (act1, act2, act3, act4):
                    a(n)
                    a(n + 1)

            def ev_at(i, k):
                t = 2 * i + k
                act.wait_ge(q["a_at"], t + 1)
                after(act, q["a_wo"], t)
                copy(attT.rearrange("p k t -> p (k t)"), ps[:, 7, 0:D]).then_inc(q["a_atT"], 1)

            def ev_q(i, k):
                t = 2 * i + k
                act.wait_ge(q["a_qm"], t + 1)
                after(act, q["a_sc"], 3 * t - 3)
                copy(qT[k % 2].rearrange("p k t -> p (k t)"), ps[:, 5, 0:D]).then_inc(q["a_q"], 1)

            def step1(i, k, p1=True, p2=True, nxt=True):
                if p1:
                    ev_pt(i, k - 1, "a", (0, 1))
                if p2:
                    ev_at(i, k - 2)
                if nxt:
                    ev_xt(i, k + 1, "a", "a_qm")
                if p1:
                    ev_pt(i, k - 1, "a", (2,))
                exps(i, k, "a", HD ** -0.5)
                if nxt:
                    ev_q(i, k + 1)

            ev_xt(0, 0, "a", "a_qm")
            ev_q(0, 0)
            step1(0, 0, p1=False, p2=False)
            step1(0, 1, p2=False)
            step1(1, 0)
            step1(1, 1)
            with act.Fori(2, TB - 1) as i:
                step1(i, 0)
                step1(i, 1)
            step1(TB - 1, 0)
            step1(TB - 1, 1, nxt=False)
            ev_pt(TB - 1, 1, "a")
            ev_at(TB - 1, 0)

            def ev_router(o, bank):
                for m in range(KD):
                    act.wait_ge(q["r_tx"], 2 * o + m + 1)
                    copy(xT[o][:, m, :], ps[:, bank + m, :]).then_inc(q["r_ev"], 1)

            ev_router(0, 0)
            ev_at(TB - 1, 1)
            ev_router(1, 2)

            def s_silu(o, f):
                n = 4 * o + f
                act.wait_ge(q["s_h"], 2 * n + 1)
                after(act, q["s_hs"], n)
                nc.scalar.activation(sil_s, ps[:, 2 * (f % 2), :], ACT.Silu).then_inc(q["s_sil"], 1)

            s_silu(0, 0)
            s_silu(0, 1)
            act.wait_ge(q["a_wo"], T)
            ev_router(2, 6)
            ev_router(3, 4)
            s_silu(0, 2)
            s_silu(0, 3)
            act.wait_ge(q["r_esc"], 1)
            nc.scalar.activation(esc[:], esc[:], ACT.Exp).then_inc(q["r_e"], 1)
            for o in range(1, NG):
                for f in range(FC):
                    s_silu(o, f)

            def e_xt(i, k):
                s = 2 * i + k
                act.wait_ge(q["e_tx"], s + 1)
                after(act, q["e_h"], 2 * (s - 1))
                copy(xgT[k % 2].rearrange("p k t -> p (k t)"), ps[:, 4, 0:D]).then_inc(q["e_xt"], 1)

            def e_ht(i, k):
                s = 2 * i + k
                act.wait_ge(q["e_th"], 2 * s + 1)
                after(act, q["e_y"], s - 1)
                copy(hT[k % 2][:, 0:2, :].rearrange("p f t -> p (f t)"), ps[:, 5, 0:2 * P]).then_inc(q["e_hTa"], 1)

            def e_silu(i, k):
                s = 2 * i + k
                act.wait_ge(q["e_h"], 2 * s + 1)
                after(act, q["e_hh"], s - 1)
                nc.scalar.activation(sil[k % 2], ps[:, 2 * (k % 2), :], ACT.Silu).then_inc(q["e_sil"], 1)

            def e_step(i, k, prev=True, nxt=True):
                if prev:
                    e_ht(i, k - 1)
                if nxt:
                    e_xt(i, k + 1)
                e_silu(i, k)

            e_xt(0, 0)
            e_step(0, 0, prev=False)
            e_step(0, 1)
            e_step(1, 0)
            e_step(1, 1)
            with act.Fori(2, SLOTS // 2) as i:
                e_step(i, 0)
                e_step(i, 1)
            e_step(SLOTS // 2, 0, nxt=False)
            e_ht(SLOTS // 2, 0)

        @block.vector
        def _(dve):
            v = nc.vector
            seq = Chain(dve, q["dve_seq"])

            def norm_stats(tile):
                seq.mark(v.bn_stats(stats[:, tile, :], xs[:, tile, :]))

            def norm(o, tile):
                return v.tensor_scalar(o, xs[:, tile, :], mv[:, tile, 0:1], rstd[:, tile:tile + 1]
                                       if isinstance(tile, int) else rstd[:, bass.ds(tile, 1)],
                                       ALU.subtract, ALU.mult)

            def variances(tiles=range(T)):
                seq.sync()
                for t in tiles:
                    seq.mark(v.bn_aggr(mv[:, t, :], stats[:, t, :]))
                seq.sync()
                v.tensor_scalar(vare[:], mv[:, :, 1], EPS, None, ALU.add).then_inc(q["var_done"], 1)

            seq(v.memset(kbd.rearrange("p b j n -> p (b j n)"), 0.0))
            dve.wait_ge(q["ld_par"], 16)
            for w, col in enumerate((V_BK, V_BV)):
                if w == 1:
                    dve.wait_ge(q["pool_fill"], 1)
                for u in range(3):
                    j0, j1 = 3 * u, min(3 * u + 3, PAIRS)
                    dve.wait_ge(q["su_mm"], 3 * w + u + 1)
                    for r in range(2):
                        rows = slice(64 * r, 64 * r + 64)
                        src = ps[rows, 3 * w + u, 0:PW * (j1 - j0)].rearrange("p (j b t) -> p j b t", b=B, t=NK)
                        for b in range(B):
                            if w == 0:
                                o = kbd[rows, b, j0:j1, NK * r:NK * r + NK]
                            else:
                                o = zv[rows, b, P:P + PAIRS * ZS].rearrange("p (j s) -> p j s", s=ZS)[
                                    :, j0:j1, NK * r:NK * r + NK]
                            last = v.tensor_tensor(o, src[:, :, b, :],
                                                   spread(par[rows, col + j0:col + j1], 2, [64, j1 - j0, NK]), ALU.add)
                    last.then_inc(q["su_kv"], 1)

            def bq_parts(b):
                dve.wait_ge(q["su_crow"], b + 1)
                c = crow[0:1, b, :]
                for n in range(2):
                    seq(v.tensor_copy(cb[:, n, :], c))
                    seq(v.tensor_tensor(c, c, cb[:, n, :], ALU.subtract))
                v.tensor_copy(cb[:, 2, :], c).then_inc(q["su_crow_bf"], 1)

            dve.wait_ge(q["ld_con"], 16)
            seq(v.memset(spare, 0.0))
            v.tensor_copy(spare[:, D:D + 1], con[:, C_SP:C_SP + 1]).then_inc(q["memset_done"], 1)
            seq.mark(v.memset(ones_bf[:], 1.0))
            for p in range(2):
                seq.mark(v.memset(pt[p][:, KC - 1, :], 0.0))
            seq.sync()
            for p in range(2):
                seq.mark(v.memset(pt[p][BO_ROW:BO_ROW + 1, KC - 1, :], 1.0))
            seq.mark(v.tensor_copy(up_bf[:], con[:, C_UP:C_UP + P]))
            seq.mark(v.tensor_scalar(hb[:, 0:1], par[:, V_GB3:V_GB3 + 1], 0.5, None, ALU.mult))
            seq.mark(v.tensor_scalar(hb[:, 1:2], par[:, V_CB4:V_CB4 + 1], 0.5, None, ALU.mult))
            for b in range(B):
                v.tensor_copy(va[:, b, :, :, HD],
                              con[:, C_IN:C_IN + 3 * KC].rearrange("p (c h) -> p c h", h=3)).then_inc(q["ones_done"], 1)
            dve.wait_ge(q["pool_fill"], 2)
            dve.wait_ge(q["ld_mask"], 32)
            dve.wait_ge(q["ld_con"], 16)
            seq.mark(v.tensor_scalar(mlhs[0:NK, :, :], mask_u8[:], BIG, -BIG, ALU.mult, ALU.add))
            for b in range(B):
                seq.mark(v.tensor_copy(mrhs[b][0:NK, :].rearrange("p (h t) -> p h t", h=H),
                                       spread(ident[0:NK, 0:NK], 1, [NK, H, NK])))
            seq.sync()
            v.memset(den[:], 0.0).then_inc(q["mask_done"], 1)
            bq_parts(0)
            dve.wait_ge(q["ld_x"], 64)
            for t in range(T):
                seq.mark(v.bn_stats(stats[:, t, :], xs[:, t, :]))
            seq.sync()
            variances()
            pads = [(0, ZL), (ZL + HALF, Z1)]
            for a, z in pads:
                seq.mark(v.memset(z1[:, :, :, a:z], 0.0))
            for w in range(2):
                dve.wait_ge(q["su1_mm"], w + 1)
                src = ps[:, 3 + w, 0:2 * PW].rearrange("p (m b t) -> p m b t", m=2, b=B)
                for b in range(B):
                    for m in range(2):
                        o = kb1[:, b, m, :] if w == 0 else z1[:, b, m, ZL:ZL + HALF]
                        last = v.tensor_tensor(o.rearrange("p (h t) -> p h t", h=8), spread(src[:, m, b, :], 1, [P, 8, NK]),
                                               spread(con[:, C_BD:C_BD + 8], 2, [P, 8, NK]), ALU.mult)
                last.then_inc(q["su1_dve"], 1)
            dve.wait_ge(q["rstd_done"], 1)
            norm(xn[0], 0).then_inc(q["n_xn"], 1)
            norm(xn[1], TB).then_inc(q["n_xn"], 1)
            dve.wait_ge(q["ld_crow"], 48)
            bq_parts(1)
            def soft(i, k, pre):
                t = 2 * i + k
                after(dve, q[pre + "_tp"], 3 * t - 3)
                for u, (a, z) in enumerate(UNITS):
                    dve.wait_ge(q[pre + "_sc"], 3 * t + u + 1)
                    n = z - a
                    src = ps[:, u, 0:NK * n].rearrange("p (h t) -> p h t", h=n)
                    seq(v.tensor_reduce(mx[:, a:z], src, AX.X, ALU.max))
                    v.tensor_tensor(sc[k % 2][:, NK * a:NK * z].rearrange("p (h t) -> p h t", h=n), src,
                                    spread(mx[:, a:z], 2, [P, n, NK]), ALU.subtract).then_inc(q[pre + "_sub"], 1)

            def xn0(i, k, pre):
                t = 2 * i + k
                after(dve, q[pre + "_tx"], t - 1)
                norm(xn[k % 2], tile_of(i, k)).then_inc(q[pre + "_xn"], 1)

            def step0(i, k, prev=True, nxt=True):
                soft(i, k, "n")
                dve.wait_ge(q["n_exp"], 2 * i + k + 1)
                s3 = sc[k % 2].rearrange("p (h t) -> p h t", h=H)
                seq(v.tensor_reduce(den[:], s3, AX.X, ALU.add))
                seq(v.reciprocal(rden[:], den[:]))
                v.tensor_tensor(s3, s3, spread(rden[:], 2, [P, H, NK]), ALU.mult).then_inc(q["n_p"], 1)
                if prev:
                    res0(i, k - 1)
                if nxt:
                    xn0(i, k + 2, "n")
                if prev:
                    norm_stats(tile_of(i, k - 1))

            def res0(i, k):
                tile = tile_of(i, k)
                dve.wait_ge(q["n_pv"], 2 * i + k + 1)
                ins = v.tensor_tensor(xs[:, tile, :], xs[:, tile, :], ps[:, 6 + k % 2, 0:D], ALU.add)
                ins.then_inc(q["n_res"], 1)
                dve.wait_ge(q["n_res"], 2 * i + k + 1)

            dve.wait_ge(q["gate_done"], 1)
            dve.wait_ge(q["ld_bo"], 16 * B)
            v.tensor_scalar(vo[BO_ROW:BO_ROW + 1, :, KC - 1, :], vo[BO_ROW:BO_ROW + 1, :, KC - 1, :],
                            gate[BO_ROW:BO_ROW + 1, 0:1], None, ALU.mult).then_inc(q["bo_done"], 1)

            step0(0, 0, prev=False)
            seq(v.tensor_scalar(mrf[:], mrow_u8[:], BIG, -BIG, ALU.mult, ALU.add))
            seq(v.tensor_reduce(mval[:, 0:2], mrow_u8[:], AX.X, ALU.add))
            seq(v.reciprocal(mval[:, 2:4], mval[:, 0:2]))
            seq(v.tensor_scalar(mval[:, 0:2], mval[:, 2:4], 0.0, None, ALU.mult))
            for b in range(B):
                seq.mark(v.tensor_scalar(mrow[b][:].rearrange("p (h t) -> p h t", h=H),
                                         spread(mrf[:, b, :], 1, [1, H, NK]), mval[:, b:b + 1], None, ALU.add))
            seq.sync()
            v.memset(den[:], 0.0).then_inc(q["mrow_done"], 1)
            step0(0, 1)
            step0(1, 0)
            step0(1, 1)
            with dve.Fori(2, TB - 1) as i:
                seq.enter(i - 2, 12)
                step0(i, 0)
                step0(i, 1)
            seq.leave(TB - 3)
            def normed(count, tiles, o, ready):
                dve.wait_ge(q["rstd_done"], count)
                for t in tiles:
                    norm(o(t), t).then_inc(q[ready], 1)

            pair_tiles = [[4 * ffn_group(n) + j for n in (2 * p, 2 * p + 1) for j in range(4)] for p in range(2)]
            step0(TB - 1, 0, nxt=False)
            variances(pair_tiles[0])
            normed(2, pair_tiles[0], lambda t: xng[:, t // 4, t % 4, :], "f_xn")
            step0(TB - 1, 1, nxt=False)
            res0(TB - 1, 1)
            norm_stats(T - 1)

            variances(pair_tiles[1])
            normed(3, pair_tiles[1], lambda t: xng[:, t // 4, t % 4, :], "f_xn")
            sgn = con[:, C_SG:C_SG + 1]
            seq(v.tensor_scalar(cpl[:, 3:4], par[:, V_AR:V_AR + 1], 0.7, None, ALU.mult))
            seq.mark(v.tensor_scalar(cpl[:, 0:1], par[:, V_AR:V_AR + 1], 0.3, sgn, ALU.mult, ALU.mult))
            dve.wait_ge(q["f_upd"], NG)
            cv = csum[:].rearrange("p m (b h) -> p m b h", h=2)
            seq(v.tensor_tensor(gcx[:], cv[:, :, :, 0], cv[:, :, :, 1], ALU.add))
            v.tensor_scalar(gcx[:], gcx[:], 1.0 / S, None, ALU.mult).then_inc(q["f_gcx"], 1)
            dve.wait_ge(q["f_gact"], 3)
            seq(v.tensor_scalar(cpl[:, 1:3], gtan[:], cpl[:, 3:4], 0.1, ALU.mult, ALU.add))
            seq(v.tensor_scalar(cpl[:, 1:3], cpl[:, 1:3], sgn, None, ALU.mult))

            def update(n):
                g, b = ffn_group(n), n % 2
                dve.wait_ge(q["f_a4"], n + 1)
                x0, x1 = st_x[:, 0, g, :], st_x[:, 1, g, :]
                seq(v.tensor_scalar(cs, tt[b], cpl[:, 0:1], cpl[:, 1 + b:2 + b], ALU.mult, ALU.add))
                seq.mark(v.tensor_tensor(u0, cs, x1, ALU.mult))
                seq(v.tensor_tensor(u1, cs, x0, ALU.mult))
                v.tensor_tensor(x0, x0, u0, ALU.add)
                v.tensor_tensor(x1, x1, u1, ALU.subtract).then_inc(q["f_upd"], 1)
                dve.wait_ge(q["f_upd"], n + 5)

            def ffn_out(n, banks):
                for u in range(2):
                    t = 4 * ffn_group(n) + 2 * u
                    dve.wait_ge(q["f_bt"], 2 * n + u + 1)
                    xx = xs[:, t:t + 2, :].rearrange("p t d -> p (t d)")
                    v.scalar_tensor_tensor(xx, ps[:, banks[u], :], gate[:, 2:3], xx, ALU.mult,
                                           ALU.add).then_inc(q["f_res"], 1)
                    dve.wait_ge(q["f_res"], 2 * n + u + 1)
                    norm_stats(t)
                    norm_stats(t + 1)

            for n in range(10):
                update(n)
            ffn_out(0, (3, 7))
            ffn_out(1, (0, 1))
            variances(pair_tiles[0])
            dve.wait_ge(q["rstd_done"], 4)

            def att1(i, k):
                t = 2 * i + k
                dve.wait_ge(q["a_pv"], t + 1)
                o = ps[:, 6, 0:H * (HD + 1)].rearrange("p (h e) -> p h e", e=HD + 1)
                seq(v.reciprocal(rden[:], o[:, :, HD]))
                after(dve, q["a_at"], t)
                v.tensor_tensor(att.rearrange("p (h e) -> p h e", e=HD), o[:, :, 0:HD],
                                spread(rden[:], 2, [P, H, HD]), ALU.mult).then_inc(q["a_att"], 1)

            def res1(i, k):
                tile = tile_of(i, k)
                dve.wait_ge(q["a_wo"], 2 * i + k + 1)
                v.scalar_tensor_tensor(xs[:, tile, :], ps[:, 7, 0:D], gate[:, 1:2], xs[:, tile, :],
                                       ALU.mult, ALU.add).then_inc(q["a_res"], 1)
                dve.wait_ge(q["a_res"], 2 * i + k + 1)

            def step1(i, k, p1=True, p3=True, nxt=True):
                if p3:
                    res1(i, k - 3)
                soft(i, k, "a")
                if p1:
                    att1(i, k - 1)
                if p3:
                    norm_stats(tile_of(i, k - 3))
                if nxt:
                    xn0(i, k + 2, "a")

            xn0(0, 0, "a")
            xn0(0, 1, "a")
            update(10)
            update(11)
            step1(0, 0, p1=False, p3=False)
            ffn_out(2, (3, 4))
            ffn_out(3, (6, 7))
            variances(pair_tiles[1])
            dve.wait_ge(q["rstd_done"], 5)
            step1(0, 1, p3=False)
            step1(1, 0, p3=False)
            step1(1, 1)
            with dve.Fori(2, TB - 1) as i:
                seq.enter(i - 2, 10)
                step1(i, 0)
                step1(i, 1)
            seq.leave(TB - 3)
            tiles_of = [[t + j for t in GROUPS[2 * n:2 * n + 2] for j in range(4)] for n in range(2)]

            step1(TB - 1, 0, nxt=False)
            variances(tiles_of[0])
            step1(TB - 1, 1, nxt=False)
            res1(TB - 1, -1)
            norm_stats(tile_of(TB - 1, -1))
            normed(6, tiles_of[0], lambda t: xn4[:, t, :], "r_xn")
            att1(TB - 1, 1)
            for k in range(2):
                res1(TB - 1, k)
                norm_stats(tile_of(TB - 1, k))
            variances(tiles_of[1])

            def logits_in(n):
                dve.wait_ge(q["r_lg"], 2 * n + 2)
                lg4 = lg[:].rearrange("p (a b t) e -> p a b t e", a=2, b=2)[:, :, n, :, :]
                v.tensor_copy(lg4, ps[:, 5 + n, 0:8 * NE].rearrange("p (a t e) -> p a t e", a=2, e=NE)
                              ).then_inc(q["r_lgc"], 1)
                dve.wait_ge(q["r_lgc"], n + 1)

            def s_prod(o, f):
                n = 4 * o + f
                dve.wait_ge(q["s_h"], 2 * n + 2)
                dve.wait_ge(q["s_sil"], n + 1)
                after(dve, q["s_y"], 2 * o)
                v.tensor_tensor(hs[:, f, :], sil_s, ps[:, 2 * (f % 2) + 1, :], ALU.mult).then_inc(q["s_hs"], 1)

            def s_out(o, u):
                dve.wait_ge(q["s_y"], 2 * o + u + 1)
                t = GROUPS[o] + 2 * u
                xx = xs[:, t:t + 2, :].rearrange("p t d -> p (t d)")
                v.scalar_tensor_tensor(xx, ps[:, 4 + u, :], gw[:, 0:1], xx, ALU.mult, ALU.add).then_inc(q["s_res"], 1)
                dve.wait_ge(q["s_res"], 2 * o + u + 1)

            full = [P, T, NE]
            rev = spread(con[:, C_RE:C_RE + NE], 1, full)

            def one_hot(o, scores, top):
                seq(v.tensor_reduce(top[:], scores[:], AX.X, ALU.max))
                seq(v.tensor_tensor(ra[:], scores[:], spread(top[:], 2, full), ALU.is_equal))
                seq(v.tensor_tensor(ra[:], ra[:], rev, ALU.mult))
                seq(v.tensor_reduce(r1[:], ra[:], AX.X, ALU.max))
                seq(v.tensor_tensor(o[:], ra[:], spread(r1[:], 2, full), ALU.is_equal))

            flat = "p t e -> p (t e)"

            def scans():
                dve.wait_ge(q["r_rank"], 2)
                seq(v.tensor_copy(tot[0][:], ps[:, 7, 0:T * NE].rearrange("p (t e) -> p t e", e=NE)))
                cur, step = 0, 1
                while step < T:
                    seq.mark(v.tensor_copy(tot[1 - cur][:, 0:step, :], tot[cur][:, 0:step, :]))
                    seq(v.tensor_tensor(tot[1 - cur][:, step:, :], tot[cur][:, step:, :], tot[cur][:, 0:T - step, :],
                                        ALU.add))
                    cur, step = 1 - cur, 2 * step
                return cur

            def slots(cur):
                seq(v.tensor_tensor(cmp_[:], spread(tot[cur][:, T - 1, :], 2, [P, NE, T]),
                                    spread(con[:, C_TH:C_TH + T], 1, [P, NE, T]), ALU.is_gt))
                seq(v.tensor_reduce(ntl[:], cmp_[:], AX.X, ALU.add))
                seq(v.tensor_copy(bs[0][:], ntl[:]))
                b0, step = 0, 1
                while step < NE:
                    seq.mark(v.tensor_copy(bs[1 - b0][:, 0:step], bs[b0][:, 0:step]))
                    seq(v.tensor_tensor(bs[1 - b0][:, step:], bs[b0][:, step:], bs[b0][:, 0:NE - step], ALU.add))
                    b0, step = 1 - b0, 2 * step
                seq(v.tensor_tensor(cnt[:], bs[b0][:], ntl[:], ALU.subtract))
                seq(v.tensor_scalar(cnt[:], cnt[:], float(P), None, ALU.mult))
                seq(v.tensor_tensor(rank[:], ps[:, 6, 0:T * NE].rearrange("p (t e) -> p t e", e=NE),
                                    spread(cnt[:], 1, full), ALU.add))
                seq(v.tensor_tensor(rank[:, 1:, :], rank[:, 1:, :], tot[cur][:, 0:T - 1, :], ALU.add))
                for k in range(2):
                    seq(v.tensor_tensor(ra[:], rank[:], oh[k][:], ALU.mult))
                    seq(v.tensor_reduce(pos[:], ra[:], AX.X, ALU.add))
                    v.tensor_copy(idx[k][:], pos[:]).then_inc(q["r_pos"], 1)
                    dve.wait_ge(q["r_pos"], k + 1)
                seq(v.tensor_tensor(scmp[:], spread(bs[b0][:], 1, [P, SLOTS, NE]),
                                    spread(con[:, C_SL:C_SL + SLOTS], 2, [P, SLOTS, NE]), ALU.is_le))
                seq(v.tensor_reduce(sexp[:], scmp[:], AX.X, ALU.add))
                seq(v.tensor_scalar(sei[:], sexp[:], float(NE - 1), None, ALU.min))

            def route_weights():
                dve.wait_ge(q["r_e"], 1)
                seq(v.tensor_copy(trow[:, :, D], con[:, C_TK:C_TK + T]))
                seq(v.tensor_reduce(esum[:], esc[:], AX.X, ALU.add))
                seq(v.reciprocal(ersum[:], esum[:]))
                for k in range(2):
                    seq(v.tensor_tensor(ra[:], esc[:], oh[k][:], ALU.mult))
                    seq(v.tensor_reduce(wt[k][:], ra[:], AX.X, ALU.add))
                    seq(v.tensor_tensor(wt[k][:], wt[k][:], ersum[:], ALU.mult))
                    if k == 0:
                        v.tensor_scalar(trow[:, :, D + 1], wt[k][:], gw[:, 1:2], None, ALU.mult).then_inc(q["r_row"], 1)

            logits_in(0)
            normed(7, tiles_of[1], lambda t: xn4[:, t, :], "r_xn")
            s_prod(0, 0)
            seq.mark(v.tensor_scalar(gw[:, 0:1], gate[:, 3:4], 1.0 / 3.0, None, ALU.mult))
            seq(v.tensor_scalar(gw[:, 1:2], gate[:, 3:4], 2.0 / 3.0, None, ALU.mult))
            s_prod(0, 1)
            s_prod(0, 2)
            logits_in(1)
            one_hot(oh[0], lg, m1)
            v.tensor_tensor(esc[:], lg[:], spread(m1[:], 2, full), ALU.subtract).then_inc(q["r_esc"], 1)
            s_prod(0, 3)
            seq(v.scalar_tensor_tensor(lg2[:].rearrange(flat), oh[0][:].rearrange(flat), -BIG,
                                       lg[:].rearrange(flat), ALU.mult, ALU.add))
            one_hot(oh[1], lg2, m2)
            v.tensor_tensor(msk[:], oh[0][:], oh[1][:], ALU.add).then_inc(q["r_mask"], 1)
            s_out(0, 0)
            cur = scans()
            slots(cur)
            s_out(0, 1)
            route_weights()
            s_prod(1, 0)
            s_prod(1, 1)
            s_prod(1, 2)
            s_prod(1, 3)
            s_out(1, 0)
            s_out(1, 1)
            for f in range(FC):
                s_prod(2, f)
                if f == 2:
                    dve.wait_ge(q["r_scat0"], T * 16)
                    v.tensor_scalar(trow[:, :, D + 1], wt[1][:], gw[:, 1:2], None, ALU.mult).then_inc(q["r_row"], 1)
            s_out(2, 0)
            s_out(2, 1)
            for f in range(FC):
                s_prod(3, f)
            s_out(3, 0)
            s_out(3, 1)

            def e_meta(i, k):
                s = 2 * i + k
                dve.wait_ge(q[f"e_ld{k}"], 16 * (i + 1))
                v.tensor_copy(slot_meta[:, bass.ds(s, 1), :].rearrange("p a n -> p (a n)"),
                              xg[k][:, D:RW]).then_inc(q["e_meta"], 1)

            def e_ht(i, k):
                s = 2 * i + k
                dve.wait_ge(q["e_th"], 2 * s + 2)
                after(dve, q["e_y"], s - 1)
                v.tensor_copy(hT[k % 2][:, 2:4, :].rearrange("p f t -> p (f t)"),
                              ps[:, 6, 0:2 * P]).then_inc(q["e_hTv"], 1)

            def e_hh(i, k):
                s = 2 * i + k
                dve.wait_ge(q["e_h"], 2 * s + 2)
                dve.wait_ge(q["e_sil"], s + 1)
                after(dve, q["e_th"], 2 * s - 2)
                v.tensor_tensor(hh[k % 2], sil[k % 2], ps[:, 2 * (k % 2) + 1, :], ALU.mult).then_inc(q["e_hh"], 1)

            def e_y(i, k):
                s = 2 * i + k
                after(dve, q["e_add"], 16 * (s - 1))
                meta = slot_meta[:, bass.ds(s, 1), :].rearrange("p a n -> p (a n)")
                v.tensor_copy(to[k % 2][:], meta[:, 0:1]).then_inc(q["e_to"], 1)
                dve.wait_ge(q["e_y"], s + 1)
                dve.wait_ge(q["e_to"], s + 1)
                v.tensor_scalar(yo[k % 2], ps[:, 7, 0:D], meta[:, 1:2], None, ALU.mult).then_inc(q["e_yc"], 1)

            def e_step(i, k, p1=True, p2=True):
                if p1:
                    e_ht(i, k - 1)
                e_meta(i, k)
                e_hh(i, k)
                if p2:
                    e_y(i, k - 2)

            e_step(0, 0, p1=False, p2=False)
            e_step(0, 1, p2=False)
            e_step(1, 0)
            e_step(1, 1)
            with dve.Fori(2, SLOTS // 2) as i:
                e_step(i, 0)
                e_step(i, 1)
            e_step(SLOTS // 2, 0)
            e_ht(SLOTS // 2, 0)
            e_y(SLOTS // 2, -1)
            e_y(SLOTS // 2, 0)


def kernel(**inputs):
    import numpy as np
    import concourse.bacc as bacc
    from concourse.bass_utils import run_bass_kernel_spmd as run

    a = {k: np.asarray(v) for k, v in inputs.items()}

    con = np.zeros((P, C_N), np.float32)
    row = np.arange(P)
    con[:, C_ID:C_ID + P] = np.eye(P)
    con[:, C_UP:C_UP + P] = row[:, None] < row[None, :]
    con[:, C_BD:C_BD + 8] = row[:, None] // HD == np.arange(8)[None, :]
    for c in range(KC):
        h0, n = heads_of(c)
        for j in range(n):
            con[:, C_IN + 3 * c + j] = (c * P + row) // NK == h0 + j
    con[:, C_RE:C_RE + NE] = NE - np.arange(NE)
    con[:, C_TH:C_TH + T] = P * np.arange(T)
    con[:, C_SL:C_SL + SLOTS] = np.arange(SLOTS)
    con[:, C_SG] = np.where(row < 64, 1.0, -1.0)
    con[:, C_TK:C_TK + T + 1] = row[:, None] + P * np.arange(T + 1)

    small = np.zeros((P, V_N), np.float32)
    small[:, V_GX:V_GX + 2] = a["g_xattn"]
    small[:, V_GF:V_GF + 2] = a["g_ffn"]
    small[:, V_AR] = a["L0_ffn_adaptive_range"]
    small[:, V_GB3] = a["L0_ffn_gc_b3"]
    small[:, V_CB4] = a["L0_ffn_cn_b4"]
    small[:, V_CB1:V_CB1 + 2] = a["L0_ffn_cn_b1"].reshape(2, P).T
    small[:, V_CB2] = a["L0_ffn_cn_b2"]
    small[:64, V_CB3] = a["L0_ffn_cn_b3"]
    small[:, V_GB1] = a["L0_ffn_gc_b1"]
    small[:64, V_GB2] = a["L0_ffn_gc_b2"]
    for col, name in ((V_BK, "L0_xattn_bk"), (V_BV, "L0_xattn_bv"), (V_BQ, "L0_xattn_bq")):
        small[:, col:col + PAIRS] = a[name].reshape(PAIRS, P).T

    def columns(w):
        return w.transpose(1, 0, 2).reshape(D, H * DK)

    arrays = {
        "x": a["x"].reshape(B * S, D),
        "ctxT": a["ctx_1024"].reshape(B * NK, KD, P).transpose(2, 1, 0),
        "maskT": a["mask_BxSxS2_bk1"].transpose(2, 0, 1),
        "mask1": a["mask_BxS2_bk1"].reshape(1, B, NK),
        "consts": con, "small": small,
        "wk0": columns(a["L0_xattn_wk"]), "wv0": columns(a["L0_xattn_wv"]),
        "wq0T": a["L0_xattn_wq"].transpose(0, 2, 1).reshape(H * DK, D),
        "wo0": a["L0_xattn_wo"], "bo0": a["L0_xattn_bo"].reshape(1, D),
        "cw1": a["L0_ffn_cn_w1"], "cw2": a["L0_ffn_cn_w2"], "cw3": a["L0_ffn_cn_w3"],
        "cw4": np.broadcast_to(a["L0_ffn_cn_w4"], (64, P)),
        "gw1": a["L0_ffn_gc_w1"], "gw2": a["L0_ffn_gc_w2"], "gw3": np.broadcast_to(a["L0_ffn_gc_w3"], (64, P)),
        "wq1": a["L1_xattn_Wq"].T, "wk1": a["L1_xattn_Wk"].T, "wv1": a["L1_xattn_Wv"].T, "wo1": a["L1_xattn_Wo"].T,
        "wr": a["L1_ffn_w_router"], "w1": a["L1_ffn_w1"], "w3": a["L1_ffn_w3"], "w2": a["L1_ffn_w2"],
        "ws1": a["L1_ffn_ws1"], "ws3": a["L1_ffn_ws3"], "ws2": a["L1_ffn_ws2"],
    }
    nc = bacc.Bacc("TRN2", target_bir_lowering=False, num_devices=1)
    given, aps = {}, {}
    for name, value in arrays.items():
        value = np.ascontiguousarray(value)
        given[f"in_{name}"] = value
        aps[name] = nc.dram_tensor(f"in_{name}", value.shape, mybir.dt.from_np(value.dtype), kind="ExternalInput").ap()
    out = nc.dram_tensor("out_rows", (B * S + P, D), F32, kind="ExternalOutput").ap()
    build(nc, out=out, **aps)
    r = run(nc, [given], core_ids=[0])
    return r.results[0]["out_rows"][:B * S].reshape(B, S, D)
```
